# Optimizing a Trainium2 kernel written in Bass

```python
import numpy as np
import jax
import jax.numpy as jnp

def _softmax(x, axis=-1):
    return jax.nn.softmax(x, axis=axis)

def _gelu(x):
    return jax.nn.gelu(x, approximate=True)

def _silu(x):
    return jax.nn.silu(x)

def _sigmoid(x):
    return jax.nn.sigmoid(x)

def _layernorm(x, axis=-1, eps=1e-05):
    m = jnp.mean(x, axis=axis, keepdims=True)
    v = jnp.var(x, axis=axis, keepdims=True)
    return (x - m) / jnp.sqrt(v + eps)

def _scatter_add(tgt, idx, src, axis=0):
    return tgt.at[idx].add(src)

def _segment_sum(src, seg, n):
    return jax.ops.segment_sum(src, seg, n)
kernel_name = 'mk_flamingo_gated_d1_seqx_r4_343800'

def setup_inputs(seed: int=0):
    np.random.seed(seed)
    _w = jnp.asarray

    def _rec_inputs():
        import jax
        import jax.numpy as jnp
        _rk = jax.random.key(seed)
        x = 7.22e-05 + 1 * jax.random.normal(jax.random.fold_in(_rk, 1), (4, 1024, 256), jnp.float32)
        _lenS = 1024 - jax.random.randint(jax.random.fold_in(_rk, 7), (4,), 0, max(1, 1024 // 4) + 1, jnp.int32)
        _lenS2 = 77 - jax.random.randint(jax.random.fold_in(_rk, 8), (4,), 0, max(1, 77 // 4) + 1, jnp.int32)
        _ctx_1024P = jax.random.normal(jax.random.fold_in(_rk, 11), (4, 16, 256), jnp.float32)
        _ctx_1024c = jax.random.dirichlet(jax.random.fold_in(_rk, 511), 0.3 * jnp.ones((16,), jnp.float32), (4, 77))
        _ctx_1024t = jnp.einsum('bsk,bkd->bsd', _ctx_1024c, _ctx_1024P)
        _ctx_1024t = _ctx_1024t * jax.lax.rsqrt(jnp.mean(jnp.square(_ctx_1024t)) + 1e-12) * 0.953939
        ctx_1024 = 4.13588e-05 + 0.999923 * (_ctx_1024t + 0.3 * jax.random.normal(jax.random.fold_in(_rk, 611), (4, 77, 256), jnp.float32))
        _g = jax.random.normal(jax.random.fold_in(_rk, 9001), (2, 1), jnp.float32)
        _g = jnp.sign(_g) * jnp.maximum(jnp.abs(_g), 1.0) + (_g == 0) * 1.0
        g_xattn = _g[0]
        g_ffn = _g[1]
        return (x, ctx_1024, g_xattn, g_ffn)
    x, ctx_1024, g_xattn, g_ffn = _rec_inputs()

    def _L0_xattn_setup():
        import jax, jax.numpy as jnp
        import numpy as np
        EMBED_DIM = 256
        NUM_HEADS = 16
        HEAD_DIM = EMBED_DIM // NUM_HEADS
        B, S = (4, 512)
        key = jax.random.key(seed)
        ks = jax.random.split(key, 11)
        sc = 1.0 / np.sqrt(EMBED_DIM)
        return {'query': jax.random.normal(ks[0], (B, S, EMBED_DIM), jnp.float32), 'key': jax.random.normal(ks[1], (B, S, EMBED_DIM), jnp.float32), 'value': jax.random.normal(ks[2], (B, S, EMBED_DIM), jnp.float32), 'Wq': jax.random.normal(ks[3], (EMBED_DIM, EMBED_DIM), jnp.float32) * sc, 'Wk': jax.random.normal(ks[4], (EMBED_DIM, EMBED_DIM), jnp.float32) * sc, 'Wv': jax.random.normal(ks[5], (EMBED_DIM, EMBED_DIM), jnp.float32) * sc, 'Wo': jax.random.normal(ks[6], (EMBED_DIM, EMBED_DIM), jnp.float32) * sc, 'bq': jax.random.normal(ks[7], (EMBED_DIM,), jnp.float32) * 0.01, 'bk': jax.random.normal(ks[8], (EMBED_DIM,), jnp.float32) * 0.01, 'bv': jax.random.normal(ks[9], (EMBED_DIM,), jnp.float32) * 0.01, 'bo': jax.random.normal(ks[10], (EMBED_DIM,), jnp.float32) * 0.01}
    _L0_xattn_all = _L0_xattn_setup()
    _L0_xattn_in = {k: v for k, v in _L0_xattn_all.items() if k in ('Wq', 'Wk', 'Wv', 'Wo', 'bq', 'bk', 'bv', 'bo')}
    del _L0_xattn_all

    def _L0_ffn_setup():
        import jax, jax.numpy as jnp
        import numpy as np
        TOP_K = 2
        key = jax.random.key(seed)
        kx, kg, k1, k2 = jax.random.split(key, 4)
        B, T, D, E, H = (4, 256, 256, 8, 512)
        x = jax.random.normal(kx, (B, T, D), dtype=jnp.float32)
        Wg = jax.random.normal(kg, (D, E), dtype=jnp.float32) * 0.02
        W1 = jax.random.normal(k1, (E, D, H), dtype=jnp.float32) * 0.02
        W2 = jax.random.normal(k2, (E, H, D), dtype=jnp.float32) * 0.02
        return {'x': x, 'Wg': Wg, 'W1': W1, 'W2': W2}
    _L0_ffn_all = _L0_ffn_setup()
    _L0_ffn_in = {k: v for k, v in _L0_ffn_all.items() if k in ('Wg', 'W1', 'W2')}
    del _L0_ffn_all
    return {'x': x, 'ctx_1024': ctx_1024, 'g_xattn': g_xattn, 'g_ffn': g_ffn, 'L0_xattn_Wq': _L0_xattn_in['Wq'], 'L0_xattn_Wk': _L0_xattn_in['Wk'], 'L0_xattn_Wv': _L0_xattn_in['Wv'], 'L0_xattn_Wo': _L0_xattn_in['Wo'], 'L0_xattn_bq': _L0_xattn_in['bq'], 'L0_xattn_bk': _L0_xattn_in['bk'], 'L0_xattn_bv': _L0_xattn_in['bv'], 'L0_xattn_bo': _L0_xattn_in['bo'], 'L0_ffn_Wg': _L0_ffn_in['Wg'], 'L0_ffn_W1': _L0_ffn_in['W1'], 'L0_ffn_W2': _L0_ffn_in['W2']}

def reference(x, ctx_1024, g_xattn, g_ffn, L0_xattn_Wq, L0_xattn_Wk, L0_xattn_Wv, L0_xattn_Wo, L0_xattn_bq, L0_xattn_bk, L0_xattn_bv, L0_xattn_bo, L0_ffn_Wg, L0_ffn_W1, L0_ffn_W2):
    import jax
    import jax.numpy as jnp

    def _L0_xattn_ref(query, key, value, Wq, Wk, Wv, Wo, bq, bk, bv, bo):
        import jax, jax.numpy as jnp
        import numpy as np
        EMBED_DIM = 256
        NUM_HEADS = 16
        HEAD_DIM = EMBED_DIM // NUM_HEADS
        B, S = (4, 512)

        def split_heads(x):
            Bx, Sx, _ = x.shape
            return x.reshape(Bx, Sx, NUM_HEADS, HEAD_DIM).transpose(0, 2, 1, 3)
        Q = split_heads(query @ Wq + bq)
        K = split_heads(key @ Wk + bk)
        V = split_heads(value @ Wv + bv)
        scale = 1.0 / np.sqrt(HEAD_DIM).astype(np.float32)
        scores = jnp.einsum('bhqd,bhkd->bhqk', Q, K) * scale
        attn = jax.nn.softmax(scores, axis=-1)
        ctx = jnp.einsum('bhqk,bhkd->bhqd', attn, V)
        ctx = ctx.transpose(0, 2, 1, 3).reshape(query.shape[0], query.shape[1], EMBED_DIM)
        return ctx @ Wo + bo

    def _L0_ffn_ref(x, Wg, W1, W2):
        import jax, jax.numpy as jnp
        import numpy as np
        TOP_K = 2
        B, T, D = x.shape
        E = W1.shape[0]
        logits = jnp.einsum('btd,de->bte', x, Wg)
        probs = jax.nn.softmax(logits, axis=-1)
        top_w, top_i = jax.lax.top_k(probs, TOP_K)
        top_w = top_w / (jnp.sum(top_w, axis=-1, keepdims=True) + 1e-08)
        N = B * T
        oh = jax.nn.one_hot(top_i.reshape(N, TOP_K), E, dtype=x.dtype)
        combine = jnp.sum(oh * top_w.reshape(N, TOP_K)[..., None], axis=1)
        xt = x.reshape(N, D)
        h = jnp.einsum('td,edh->teh', xt, W1)
        h = jnp.square(jax.nn.relu(h))
        y = jnp.einsum('teh,ehd->ted', h, W2)
        out = jnp.einsum('te,ted->td', combine, y)
        return out.reshape(B, T, D)
    x = x + jnp.tanh(g_xattn[0]) * _L0_xattn_ref(_layernorm(x, axis=-1), ctx_1024, ctx_1024, L0_xattn_Wq, L0_xattn_Wk, L0_xattn_Wv, L0_xattn_Wo, L0_xattn_bq, L0_xattn_bk, L0_xattn_bv, L0_xattn_bo)
    x = x + jnp.tanh(g_ffn[0]) * _L0_ffn_ref(_layernorm(x, axis=-1), L0_ffn_Wg, L0_ffn_W1, L0_ffn_W2)
    return x

_drawn_inputs = setup_inputs


def setup_inputs(seed=0):
    import zlib

    import numpy as np

    out = dict(_drawn_inputs(seed))
    spreads = {}
    factors = {'L0_xattn_bq': 32.899, 'L0_xattn_bk': 64.0, 'L0_xattn_bv': 7.263, 'L0_xattn_bo': 7.387}
    for name, (base, spread) in spreads.items():
        noise = np.random.default_rng([zlib.crc32(name.encode()), seed]).standard_normal(out[name].shape)
        drawn = base * np.exp(spread * noise) if base else spread * noise
        out[name] = jnp.asarray(drawn.astype(out[name].dtype))
    for name, factor in factors.items():
        out[name] = (out[name] * factor).astype(out[name].dtype)
    return out
```

```python
from contextlib import ExitStack

import numpy as np
import concourse.bass as bass
from concourse import mybir

F32 = mybir.dt.float32
F32R = mybir.dt.float32r
I32 = mybir.dt.int32
ALU = mybir.AluOpType
ACT = mybir.ActivationFunctionType
AX = mybir.AxisListType

P = 128
B, S, D = 4, 1024, 256
KEYS = 77
HEADS, DH = 16, 16
E, H = 8, 512
EPS = 1e-5

N = B * S
NT = N // P
DC = D // P
HC = H // P
UNITS = 2 * NT
UH = HEADS // 2
UC = UH * KEYS
QH = UH // 2
QC = QH * KEYS
KC = -(-UC // P)
UPAD = KC * P
WIN = 3
VW = DH + 1
HEAD0 = [min(P * i // KEYS, UH - WIN) for i in range(KC)]
GT = 2
NG = NT // GT
GPB = NG // B
CHOICES = 2
NJ = (CHOICES * N + E * (P - 1)) // P
NC = NT * CHOICES
XBUF = 4
HW = 512


def constants():
    p = np.arange(P)[:, None]
    row = np.arange(P)[None, :]
    head = [(P * i + p) // KEYS for i in range(KC)]
    parts = {
        "ident": p == row,
        "before": p < row,
        "kmask": (p % 64) // DH == np.arange(QH)[None, :],
        "vmask": np.concatenate([head[i] == HEAD0[i] + np.arange(WIN)[None, :] for i in range(KC)], 1),
        "iota": row + 0 * p,
        "token": P * np.arange(NT)[None, :] + p,
        "spare": CHOICES * N + P * np.arange(NJ)[None, :] + p,
        "lowest": E - np.arange(E)[None, :] + 0 * p,
        "full": P * np.arange(NT)[None, :] + 0 * p,
    }
    at, cols = {}, 0
    for name, a in parts.items():
        at[name] = (cols, cols + a.shape[1])
        cols += a.shape[1]
    return np.concatenate([a.astype(np.float32) for a in parts.values()], 1), at


def build(nc, x, ctx_in, g_xattn, g_ffn, wq, wk, wv, wo, bq, bk, bv, bo, wg, w1, w2, consts, out):
    _, at = constants()
    x1_dram = nc.dram_tensor("x1_scratch", (N, D), F32).ap()
    xn2_dram = nc.dram_tensor("xn2_scratch", (N, D), F32).ap()
    y_dram = nc.dram_tensor("y_scratch", (CHOICES * N + NJ * P, D), F32).ap()

    rows = lambda a: a.rearrange("(t p) d -> p t d", p=P)
    x_rows = rows(x.rearrange("b s d -> (b s) d"))
    out_rows = rows(out.rearrange("b s d -> (b s) d"))
    x1_rows = rows(x1_dram)
    y_rows = y_dram[0:CHOICES * N, :].rearrange("(t p k) d -> p t k d", p=P, k=CHOICES)

    ctx = ExitStack()
    with ctx:
        def sem(name):
            return ctx.enter_context(nc.semaphore(name))

        def place(stack, name, shape, dt=F32):
            return stack.enter_context(nc.sbuf_tensor(name, shape, dt))

        cst = place(ctx, "cst", [P, consts.shape[1]])
        C = lambda name: cst[:, at[name][0]:at[name][1]]
        ident = C("ident")
        ones = place(ctx, "ones", [P, P])
        logits = place(ctx, "logits", [P, NT, E])
        gates = place(ctx, "gates", [P, 2])
        tg = place(ctx, "tg", [P, 2])
        w1hi = place(ctx, "w1hi", [P, E * DC * H], F32R)
        w1lo = place(ctx, "w1lo", [P, E * DC * H], F32R)
        EW = DC * H
        with ExitStack() as early:
            ctx_sb = place(early, "ctx_sb", [KEYS, B, D])
            ctxT = place(early, "ctxT", [P, DC, B, 3 * KEYS])
            wk_sb = place(early, "wk_sb", [P, DC, D])
            wv_sb = place(early, "wv_sb", [P, DC, D])
            kT = place(early, "kT", [P, DC, B * KEYS])
            kblock = place(early, "kblock", [P, B, QH, KEYS])
            bv_sb = place(early, "bv_sb", [1, D])
            wq_sb = place(early, "wq_sb", [P, DC, D])
            wo_sb = place(early, "wo_sb", [P, DC, D])
        w2hi = place(ctx, "w2hi", [P, E * HC * D], F32R)
        tile_w = place(ctx, "tile_w", [P, CHOICES, NT])
        gather_at = place(ctx, "gather_at", [P, NJ], I32)
        scatter_at = place(ctx, "scatter_at", [P, NJ], I32)
        expert_at = place(ctx, "expert_at", [1, NJ], I32)

        with ExitStack() as a:
            khi = place(a, "khi", [P, DC, B, QC], F32R)
            klo = place(a, "klo", [P, DC, B, QC], F32R)
            vals = place(a, "vals", [P, B, 2, KC, WIN * VW])
            wqhi = place(a, "wqhi", [P, DC, D], F32R)
            wqlo = place(a, "wqlo", [P, DC, D], F32R)
            wohi = place(a, "wohi", [P, DC, D], F32R)
            wolo = place(a, "wolo", [P, DC, D], F32R)
            wg_sb = place(a, "wg_sb", [P, DC, E])
            bo_sb = place(a, "bo_sb", [P, D])
            bq_sb = place(a, "bq_sb", [P, DC])
            bk_sb = place(a, "bk_sb", [P, DC])
            raw = [place(a, f"raw{i}", [P, EW]) for i in range(2)]
            xs = [place(a, f"xs{i}", [P, GT, D]) for i in range(XBUF)]
            xn = place(a, "xn", [P, GT, D])
            xnThi = place(a, "xnThi", [P, DC, GT * P], F32R)
            xnTlo = place(a, "xnTlo", [P, DC, GT * P], F32R)
            qThi = [place(a, f"qThi{i}", [P, DC, GT * P], F32R) for i in range(2)]
            qTlo = [place(a, f"qTlo{i}", [P, DC, GT * P], F32R) for i in range(2)]
            prob = [place(a, f"prob{i}", [P, UPAD]) for i in range(2)]
            probT = [place(a, f"probT{i}", [P, KC, P]) for i in range(2)]
            attn = place(a, "attn", [P, D])
            attnThi = place(a, "attnThi", [P, DC, P], F32R)
            attnTlo = place(a, "attnTlo", [P, DC, P], F32R)
            xn2 = [place(a, f"xn2{i}", [P, D]) for i in range(2)]
            xn2T = place(a, "xn2T", [P, DC, P])
            rowmax = place(a, "rowmax", [P, UH])
            recip = place(a, "recip", [P, UH])
            st1 = place(a, "st1", [P, GT, 6])
            mv1 = place(a, "mv1", [P, GT, 2])
            ve1 = place(a, "ve1", [P, GT])
            rs1 = place(a, "rs1", [P, GT])
            st2 = place(a, "st2", [P, 6])
            mv2 = place(a, "mv2", [P, 2])
            ve2 = place(a, "ve2", [P, 1])
            rs2 = place(a, "rs2", [P, 1])
            half = place(a, "half", [P, GT])
        w2lo = place(ctx, "w2lo", [P, E * HC * D], F32R)
        with ExitStack() as r:
            raw2 = [place(r, f"raw2{i}", [P, EW]) for i in range(2)]
            PART = NT // 2
            onehot_row = [place(r, f"onehot_row{i}", [P, PART, P], F32R) for i in range(2)]
            onehot_tile = [place(r, f"onehot_tile{i}", [P, PART, 2 * NJ], F32R) for i in range(2)]
            ended = place(r, "ended", [1, NJ, E - 1])
            TE = [P, NT, E]
            lgm = place(r, "lgm", TE)
            prob8 = place(r, "prob8", TE)
            pick = [place(r, f"pick{i}", TE) for i in range(CHOICES)]
            count = [place(r, f"count{i}", TE) for i in range(2)]
            slot_te = place(r, "slot_te", TE)
            totals = lgm
            top = place(r, "top", [P, CHOICES, NT])
            small = place(r, "small", [P, 4, NT])
            slot = place(r, "slot", [P, CHOICES, NT])
            slot_i = place(r, "slot_i", [P, NC], I32)
            srow_i = place(r, "srow_i", [P, NC], I32)
            stile_i = place(r, "stile_i", [P, NC], I32)
            srow = place(r, "srow", [P, NC])
            stile = place(r, "stile", [P, NC])
            need = place(r, "need", [P, E])
            first = [place(r, f"first{i}", [P, E]) for i in range(2)]
            base = place(r, "base", [P, E])
            listed = place(r, "listed", [P, 2 * NJ])
            listf = place(r, "listf", [P, 3, NJ])
        with ExitStack() as m:
            x1_all = place(m, "x1_all", [P, NT, D])
            xg = [place(m, f"xg{i}", [P, D]) for i in range(3)]
            xgThi = [place(m, f"xgThi{i}", [P, DC, P], F32R) for i in range(2)]
            xgTlo = [place(m, f"xgTlo{i}", [P, DC, P], F32R) for i in range(2)]
            hrelu = place(m, "hrelu", [P, H])
            hsq = place(m, "hsq", [P, H])
            hThi = place(m, "hThi", [P, HC, P], F32R)
            hTlo = place(m, "hTlo", [P, HC, P], F32R)
            y_sb = [place(m, f"y_sb{i}", [P, D]) for i in range(2)]
            CT = 4
            y_in = [place(m, f"y_in{i}", [P, CT, CHOICES, D]) for i in range(3)]

        bank = [ctx.enter_context(nc.psum_tensor(f"bank{i}", [P, HW], F32)) for i in range(8)]
        score_bank = [[bank[0], bank[1]], [bank[2], bank[3]]]
        t_bank = [bank[4], bank[5]]
        v_bank = bank[6]
        m_bank = bank[7]

        d_const, d_ctx, d_wkv, d_wqo, d_bias, d_gate = (sem("d_" + n) for n in ("const", "ctx", "wkv", "wqo", "bias", "gate"))
        d_x = [sem(f"d_x{i}") for i in range(XBUF)]
        d_x1 = [sem(f"d_x1{i}") for i in range(XBUF)]
        d_xn2 = [sem(f"d_xn2{i}") for i in range(2)]
        d_raw = [sem(f"d_raw{i}") for i in range(2)]
        d_raw2 = [sem(f"d_raw2{i}") for i in range(2)]
        p_w2lo, a_w2hi = sem("p_w2lo"), sem("a_w2hi")
        p_init, p_rs1, p_xb, p_rs2, p_wlo = (sem("p_" + n) for n in ("init", "rs1", "xb", "rs2", "wlo"))
        p_bo = sem("p_bo")
        t_ctx, t_k, t_v = (sem("t_" + n) for n in ("ctx", "k", "v"))
        t_xnT, t_q, t_score, t_probT, t_pv, t_attnT, t_wo, t_xn2T, t_logit = (
            sem("t_" + n) for n in ("xnT", "q", "score", "probT", "pv", "attnT", "wo", "xn2T", "logit"))
        a_tanh, a_ctxT, a_kT, a_khi, a_wqo = (sem("a_" + n) for n in ("tanh", "ctxT", "kT", "khi", "wqo"))
        a_xnT, a_q, a_exp, a_probT, a_attnT, a_xn2T, a_whi = (
            sem("a_" + n) for n in ("xnT", "q", "exp", "probT", "attnT", "xn2T", "whi"))
        v_init, v_kblock, v_klo, v_vals, v_wqo, v_var1, v_xn, v_xnT, v_q, v_sub, v_attn, v_attnT = (
            sem("v_" + n) for n in ("init", "kblock", "klo", "vals", "wqo", "var1", "xn", "xnT", "q", "sub", "attn", "attnT"))
        v_x1, v_var2, v_xn2, v_logit, v_own = (sem("v_" + n) for n in ("x1", "var2", "xn2", "logit", "own"))
        a_own, a_prob8 = sem("a_own"), sem("a_prob8")
        v_lgm, v_pick, v_row, v_tile, v_lists = (sem("v_" + n) for n in ("lgm", "pick", "row", "tile", "lists"))
        t_rank, t_list = sem("t_rank"), sem("t_list")
        d_x1all = sem("d_x1all")
        d_xg = [sem(f"d_xg{i}") for i in range(3)]
        d_ys = [sem(f"d_ys{i}") for i in range(2)]
        d_yin = [sem(f"d_yin{i}") for i in range(3)]
        d_out = sem("d_out")
        t_xgT, t_h, t_hT, t_y = (sem("t_" + n) for n in ("xgT", "h", "hT", "y"))
        a_xgT, a_relu, a_hT, a_y = (sem("a_" + n) for n in ("xgT", "relu", "hT", "y"))
        v_xgT, v_hsq, v_hT, v_out = (sem("v_" + n) for n in ("xgT", "hsq", "hT", "out"))

        SLOTS = range(-6, UNITS + 6)
        LAST_SLOT = SLOTS[-1]

        def early_step(s):
            if s % 2 and 0 <= (s - 3) // 2 < NT:
                return "attnT", (s - 3) // 2
            if s % 2 == 0 and 0 <= (s - 6) // 2 < NT:
                return "xn2T", (s - 6) // 2

        def middle_step(s):
            g = s // 4 + 1
            if s % 4 in (0, 1) and 0 <= g < NG:
                return ("xnT" if s % 4 == 0 else "q"), g

        def late_step(s):
            step = early_step(s)
            return step and ({"attnT": "wo", "xn2T": "logit"}[step[0]], step[1])

        def norm1_stats(s):
            return s // 4 + 2 if s % 4 == 2 and 0 <= s // 4 + 2 < NG else None

        def norm1_apply(s):
            return s // 4 + 2 if s % 4 == 3 and 0 <= s // 4 + 2 < NG else None

        def norm2_apply(s):
            return (s - 4) // 2 if s % 2 == 0 and 0 <= (s - 4) // 2 < NT else None

        def weight_piece(s):
            return s // 8 if s % 8 == 3 and 0 <= s // 8 < E else None

        def unit(u):
            return u if 0 <= u < UNITS else None

        shared_order = [step for s in SLOTS for step in (early_step(s), middle_step(s), late_step(s)) if step]
        drained_by = {"xnT": v_xnT, "q": v_q, "attnT": v_attnT, "wo": v_x1, "xn2T": a_xn2T, "logit": v_logit}

        def part_of(w, e):
            return w[:, e * EW:(e + 1) * EW]

        block = ctx.enter_context(nc.Block())

        @block.sync
        def _(sp):
            sp.dma_start(cst[:, :], consts).then_inc(d_const, 16)
            sp.dma_start(ctx_sb[:, :, :], ctx_in.rearrange("b k d -> k b d")).then_inc(d_ctx, 16)

            def load_x(g):
                if g >= XBUF:
                    sp.wait_ge(d_x1[g % XBUF], 16 * GT * (g // XBUF))
                    sp.wait_ge(v_xn2, GT * (g - XBUF + 1))
                sp.dma_start(xs[g % XBUF][:, :, :], x_rows[:, GT * g:GT * g + GT, :]).then_inc(d_x[g % XBUF], 16)

            load_x(0)
            sp.dma_start(wq_sb[:, :, :], wq.rearrange("(c p) n -> p c n", p=P)).then_inc(d_wqo, 16)
            load_x(1)
            sp.dma_start(wo_sb[:, :, :], wo.rearrange("(c p) n -> p c n", p=P)).then_inc(d_wqo, 16)
            sp.dma_start(wg_sb[:, :, :], wg.rearrange("(c p) n -> p c n", p=P)).then_inc(d_wqo, 16)
            load_x(2)
            load_x(3)
            for s in SLOTS:
                k = weight_piece(s)
                if k is not None:
                    if k >= 2:
                        sp.wait_ge(p_wlo, k - 1)
                    sp.dma_start(raw[k % 2][:, :].rearrange("p (c n) -> p c n", c=DC),
                                 w1[k].rearrange("(c p) n -> p c n", p=P)).then_inc(d_raw[k % 2], 16)
                late = late_step(s)
                if late and late[0] == "wo":
                    t = late[1]
                    sp.wait_ge(v_x1, t + 1)
                    sp.dma_start(x1_rows[:, t, :], xs[t // GT % XBUF][:, t % GT, :]).then_inc(d_x1[t // GT % XBUF], 16)
                t = norm2_apply(s)
                if t is not None:
                    sp.wait_ge(v_xn2, t + 1)
                    sp.dma_start(xn2_dram[t * P:(t + 1) * P, :], xn2[t % 2][:, :]).then_inc(d_xn2[t % 2], 16)
                    if t % GT == GT - 1 and t // GT + XBUF < NG:
                        load_x(t // GT + XBUF)
            sp.wait_ge(v_logit, NT)
            sp.wait_ge(p_wlo, E)
            for i in range(2):
                sp.wait_ge(d_xn2[i], 16 * (NT // 2))
            for i in range(XBUF):
                sp.wait_ge(d_x1[i], 16 * GT * (NG // XBUF))
            for k in range(E):
                if k >= 2:
                    sp.wait_ge(p_w2lo, k - 1)
                sp.dma_start(raw2[k % 2][:, :].rearrange("p (c n) -> p c n", c=HC),
                             w2[k].rearrange("(c p) n -> p c n", p=P)).then_inc(d_raw2[k % 2], 16)
            sp.wait_ge(p_w2lo, E)
            sp.wait_ge(v_lists, 1)
            sp.dma_start(x1_all[:, :, :], x1_rows).then_inc(d_x1all, 16)
            for i in range(2):
                sp.wait_ge(d_ys[i], 16 * len(range(i, NJ, 2)))
            for c in range(NT // CT):
                if c >= 3:
                    sp.wait_ge(v_out, c - 2)
                sp.dma_start(y_in[c % 3][:, :, :, :], y_rows[:, c * CT:(c + 1) * CT, :, :]).then_inc(d_yin[c % 3], 16)
            for c in range(NT // CT):
                sp.wait_ge(v_out, c + 1)
                sp.dma_start(out_rows[:, c * CT:(c + 1) * CT, :], x1_all[:, c * CT:(c + 1) * CT, :]).then_inc(d_out, 16)
            sp.wait_ge(d_out, 16 * (NT // CT))

        @block.gpsimd
        def _(pool):
            pool.memset(ones[:, :], 1.0).then_inc(p_init, 1)
            pool.memset(half[:, :], -0.5).then_inc(p_init, 1)
            pool.wait_ge(a_tanh, 1)
            pool.wait_ge(d_bias, 80)
            pool.tensor_scalar(bo_sb[:, :], bo_sb[:, :], tg[:, 0:1], None, ALU.mult).then_inc(p_bo, 1)
            pool.wait_ge(p_bo, 1)
            pool.wait_ge(p_init, 2)
            for s in SLOTS:
                g = norm1_stats(s)
                if g is not None:
                    pool.wait_ge(v_var1, g + 1)
                    pool.tensor_tensor(rs1[:, :], ve1[:, :], half[:, :], ALU.pow).then_inc(p_rs1, 1)
                t = late_step(s) and late_step(s)[0] == "wo" and late_step(s)[1]
                if late_step(s) and late_step(s)[0] == "wo":
                    pool.wait_ge(v_var2, t + 1)
                    pool.tensor_tensor(rs2[:, :], ve2[:, :], half[:, 0:1], ALU.pow).then_inc(p_rs2, 1)
                g = norm1_apply(s)
                if g is not None:
                    pool.wait_ge(v_xn, g + 1)
                    bo_b = bo_sb[:, :].unsqueeze(1).broadcast_to([P, GT, D])
                    pool.tensor_tensor(xs[g % XBUF][:, :, :], xs[g % XBUF][:, :, :], bo_b, ALU.add).then_inc(p_xb, 1)
                k = weight_piece(s)
                if k is not None:
                    pool.wait_ge(a_whi, k + 1)
                    pool.tensor_tensor(part_of(w1lo, k), raw[k % 2][:, :], part_of(w1hi, k).bitcast(F32),
                                       ALU.subtract).then_inc(p_wlo, 1)
            pool.wait_ge(v_logit, NT)
            for i in range(2):
                pool.wait_ge(d_xn2[i], 16 * (NT // 2))
            for i in range(XBUF):
                pool.wait_ge(d_x1[i], 16 * GT * (NG // XBUF))
            for k in range(E):
                pool.wait_ge(a_w2hi, k + 1)
                pool.tensor_tensor(part_of(w2lo, k), raw2[k % 2][:, :], part_of(w2hi, k).bitcast(F32),
                                   ALU.subtract).then_inc(p_w2lo, 1)
            pool.wait_ge(v_lists, 1)

            def gather(j):
                if j >= 3:
                    pool.wait_ge(t_xgT, j - 2)
                pool.indirect_dma_start(xg[j % 3][:, :], None, xn2_dram[:, :],
                                        bass.IndirectOffsetOnAxis(ap=gather_at[:, j:j + 1], axis=0)).then_inc(d_xg[j % 3], 16)

            for j in range(3):
                gather(j)
            for j in range(NJ):
                if j + 3 < NJ:
                    gather(j + 3)
                pool.wait_ge(a_y, j + 1)
                pool.indirect_dma_start(y_dram[:, :], bass.IndirectOffsetOnAxis(ap=scatter_at[:, j:j + 1], axis=0),
                                        y_sb[j % 2][:, :], None).then_inc(d_ys[j % 2], 16)

        @block.scalar
        def _(act):
            act.dma_start(gates[:, 0:1], g_xattn.partition_broadcast(P)).then_inc(d_gate, 16)
            act.dma_start(gates[:, 1:2], g_ffn.partition_broadcast(P)).then_inc(d_gate, 16)
            act.dma_start(wk_sb[:, :, :], wk.rearrange("(c p) n -> p c n", p=P)).then_inc(d_wkv, 16)
            act.dma_start(wv_sb[:, :, :], wv.rearrange("(c p) n -> p c n", p=P)).then_inc(d_wkv, 16)
            act.dma_start(bv_sb[:, :], bv.unsqueeze(0)).then_inc(d_wkv, 16)
            for c in range(DC):
                act.dma_start(bk_sb[:, c:c + 1], bk[c * P:(c + 1) * P].unsqueeze(1)).then_inc(d_bias, 16)
                act.dma_start(bq_sb[:, c:c + 1], bq[c * P:(c + 1) * P].unsqueeze(1)).then_inc(d_bias, 16)
            act.dma_start(bo_sb[:, :], bo.partition_broadcast(P)).then_inc(d_bias, 16)
            act.wait_ge(d_gate, 32)
            act.activation(tg[:, :], gates[:, :], ACT.Tanh).then_inc(a_tanh, 1)
            for c in range(DC):
                act.wait_ge(t_ctx, c + 1)
                act.activation(ctxT[:, c, :, :].rearrange("p b (r k) -> p b r k", k=KEYS),
                               bank[c][:, 0:B * KEYS].rearrange("p (b k) -> p b k", k=KEYS).unsqueeze(2)
                               .broadcast_to([P, B, 3, KEYS]), ACT.Copy).then_inc(a_ctxT, 1)
            act.wait_ge(d_bias, 80)
            for c in range(DC):
                act.wait_ge(t_k, c + 1)
                act.activation(kT[:, c, :], bank[2 + c][:, 0:B * KEYS], ACT.Identity,
                               bias=bk_sb[:, c:c + 1]).then_inc(a_kT, 1)
                act.wait_ge(v_kblock, c + 1)
                act.activation(khi[:, c, :, :], kblock[:, :, :, :].rearrange("p b h k -> p b (h k)"),
                               ACT.Copy).then_inc(a_khi, 1)
            act.wait_ge(d_wqo, 48)
            act.activation(wqhi[:, :, :], wq_sb[:, :, :], ACT.Copy).then_inc(a_wqo, 1)
            act.activation(wohi[:, :, :], wo_sb[:, :, :], ACT.Copy).then_inc(a_wqo, 1)

            for s in SLOTS:
                step = early_step(s)
                if step and step[0] == "attnT":
                    t = step[1]
                    act.wait_ge(t_attnT, t + 1)
                    act.wait_ge(t_wo, t)
                    act.activation(attnThi[:, :, :], m_bank[:, 0:D].rearrange("p (c n) -> p c n", n=P),
                                   ACT.Copy).then_inc(a_attnT, 1)
                if step and step[0] == "xn2T":
                    t = step[1]
                    act.wait_ge(t_xn2T, t + 1)
                    act.wait_ge(t_logit, t)
                    act.activation(xn2T[:, :, :], m_bank[:, 0:D].rearrange("p (c n) -> p c n", n=P),
                                   ACT.Copy).then_inc(a_xn2T, 1)
                u = unit(s + 1)
                if u is not None:
                    act.wait_ge(v_sub, u + 1)
                    act.activation(prob[u % 2][:, 0:UC], prob[u % 2][:, 0:UC], ACT.Exp,
                                   scale=DH ** -0.5).then_inc(a_exp, 1)
                step = middle_step(s)
                if step and step[0] == "xnT":
                    g = step[1]
                    act.wait_ge(t_xnT, g + 1)
                    act.wait_ge(t_q, g)
                    act.activation(xnThi[:, :, :].rearrange("p c n -> p (c n)"), m_bank[:, :], ACT.Copy).then_inc(a_xnT, 1)
                if step and step[0] == "q":
                    g = step[1]
                    act.wait_ge(t_q, g + 1)
                    if g >= 2:
                        act.wait_ge(t_score, 2 * GT * (g - 1))
                    for c in range(DC):
                        act.activation(qThi[g % 2][:, c, :], m_bank[:, c * GT * P:(c + 1) * GT * P], ACT.Identity,
                                       bias=bq_sb[:, c:c + 1]).then_inc(a_q, 1)
                u = unit(s)
                if u is not None:
                    act.wait_ge(t_probT, 2 * u + 1)
                    if u >= 2:
                        act.wait_ge(t_pv, u - 1)
                    act.activation(probT[u % 2][:, 0:3, :].rearrange("p c n -> p (c n)"), t_bank[0][:, 0:3 * P],
                                   ACT.Copy).then_inc(a_probT, 1)
                    act.wait_ge(t_probT, 2 * u + 2)
                    act.activation(probT[u % 2][:, 3:KC, :].rearrange("p c n -> p (c n)"), t_bank[1][:, 0:(KC - 3) * P],
                                   ACT.Copy).then_inc(a_probT, 1)
                k = weight_piece(s)
                if k is not None:
                    act.wait_ge(d_raw[k % 2], 16 * (k // 2 + 1))
                    act.activation(part_of(w1hi, k), raw[k % 2][:, :], ACT.Copy).then_inc(a_whi, 1)
            act.wait_ge(v_lgm, 1)
            act.activation(prob8[:, :, :], lgm[:, :, :], ACT.Exp).then_inc(a_prob8, 1)
            for k in range(E):
                act.wait_ge(d_raw2[k % 2], 16 * (k // 2 + 1))
                act.activation(part_of(w2hi, k), raw2[k % 2][:, :], ACT.Copy).then_inc(a_w2hi, 1)
            for j in range(-2, NJ):
                if 0 <= j:
                    act.wait_ge(t_hT, j + 1)
                    act.wait_ge(t_y, j)
                    act.activation(hThi[:, :, :].rearrange("p c n -> p (c n)"), bank[2 + j % 2][:, :],
                                   ACT.Copy).then_inc(a_hT, 1)
                if j + 2 < NJ:
                    i = j + 2
                    act.wait_ge(t_xgT, i + 1)
                    if i >= 2:
                        act.wait_ge(t_h, i - 1)
                    act.activation(xgThi[i % 2][:, :, :].rearrange("p c n -> p (c n)"), bank[4 + i % 2][:, 0:D],
                                   ACT.Copy).then_inc(a_xgT, 1)
                if 0 <= j + 1 < NJ:
                    i = j + 1
                    act.wait_ge(t_h, i + 1)
                    act.wait_ge(v_hsq, i)
                    act.activation(hrelu[:, :], bank[i % 2][:, :], ACT.Relu).then_inc(a_relu, 1)
                if 0 <= j:
                    act.wait_ge(t_y, j + 1)
                    if j >= 2:
                        act.wait_ge(d_ys[j % 2], 16 * (j // 2))
                    act.activation(y_sb[j % 2][:, :], bank[6 + j % 2][:, 0:D], ACT.Copy).then_inc(a_y, 1)

        @block.tensor
        def _(pe):
            def three_pass(dst, hi_l, lo_l, hi_r, lo_r, n):
                passes = [(l, r) for l, r in ((hi_l, hi_r), (hi_l, lo_r), (lo_l, hi_r))]
                for k in range(n):
                    for i, (l, r) in enumerate(passes):
                        mm = pe.matmul(dst, l(k), r(k), start=(k == 0 and i == 0), stop=(k == n - 1 and i == 2))
                return mm

            pe.wait_ge(d_const, 16)
            pe.wait_ge(d_ctx, 16)
            for c in range(DC):
                for b in range(B):
                    mm = pe.transpose(bank[c][:, b * KEYS:(b + 1) * KEYS], ctx_sb[:, b, c * P:(c + 1) * P],
                                      ident[0:KEYS, 0:KEYS])
                mm.then_inc(t_ctx, 1)
            pe.wait_ge(d_wkv, 48)
            pe.wait_ge(a_ctxT, DC)
            for c in range(DC):
                for d in range(DC):
                    mm = pe.matmul(bank[2 + c][:, 0:B * KEYS], wk_sb[:, d, c * P:(c + 1) * P],
                                   ctxT[:, d, :, 0:KEYS], start=(d == 0), stop=(d == DC - 1))
                mm.then_inc(t_k, 1)
            pe.wait_ge(p_init, 1)
            for n in range(B * KC):
                b, i = divmod(n, KC)
                if n >= 4:
                    pe.wait_ge(v_vals, n - 2)
                dst = bank[4 + n % 4][:, 0:2 * WIN * DH].rearrange("p (c n) -> p c n", c=2)
                cols = lambda w: w.rearrange("p (c h e) -> p c (h e)", c=2, e=DH)[:, :, HEAD0[i] * DH:(HEAD0[i] + WIN) * DH]
                at0 = P * i % KEYS
                for d in range(DC):
                    pe.matmul(dst, ctxT[:, d, b, at0:at0 + P], cols(wv_sb[:, d, :]), start=(d == 0), stop=False)
                pe.matmul(dst, ones[0:1, :], cols(bv_sb[:, :]), start=False, stop=True).then_inc(t_v, 1)
            pe.wait_ge(v_vals, B * KC + 1)
            pe.wait_ge(v_klo, DC)
            pe.wait_ge(v_wqo, 2)

            shared_n = [0]

            def take_shared():
                if shared_n[0]:
                    what, n = shared_order[shared_n[0] - 1]
                    pe.wait_ge(drained_by[what], n + 1)
                shared_n[0] += 1

            for s in SLOTS:
                u = unit(s + 1)
                if u is not None:
                    t, c = divmod(u, 2)
                    g = t // GT
                    pe.wait_ge(v_q, g + 1)
                    if u >= 2:
                        pe.wait_ge(v_sub, u - 1)
                    qs = slice(t % GT * P, t % GT * P + P)
                    b = g // GPB
                    for j in range(2):
                        rs = slice(64 * j, 64 * j + 64)
                        mm = three_pass(score_bank[u % 2][j][:, 0:QC],
                                        lambda k: qThi[g % 2][rs, c, qs], lambda k: qTlo[g % 2][rs, c, qs],
                                        lambda k: khi[rs, c, b, :], lambda k: klo[rs, c, b, :], 1)
                    mm.then_inc(t_score, 1)
                step = early_step(s)
                if step:
                    what, t = step
                    take_shared()
                    if what == "attnT":
                        pe.wait_ge(v_attn, 2 * t + 2)
                        src, done = attn, t_attnT
                    else:
                        pe.wait_ge(v_xn2, t + 1)
                        src, done = xn2[t % 2], t_xn2T
                    for c in range(DC):
                        mm = pe.transpose(m_bank[:, c * P:(c + 1) * P], src[:, c * P:(c + 1) * P], ident)
                    mm.then_inc(done, 1)
                u = unit(s - 1)
                if u is not None:
                    t, c = divmod(u, 2)
                    b = t // (NT // B)
                    pe.wait_ge(a_probT, 2 * u + 2)
                    if u:
                        pe.wait_ge(v_attn, u)
                    for i in range(KC):
                        mm = pe.matmul(v_bank[:, HEAD0[i] * VW:(HEAD0[i] + WIN) * VW], probT[u % 2][:, i, :],
                                       vals[:, b, c, i, :], start=(i == 0), stop=(i == KC - 1), skip_group_check=True)
                    mm.then_inc(t_pv, 1)
                step = middle_step(s)
                if step and step[0] == "xnT":
                    g = step[1]
                    take_shared()
                    pe.wait_ge(v_xn, g + 1)
                    for c in range(DC):
                        for i in range(GT):
                            mm = pe.transpose(m_bank[:, (c * GT + i) * P:(c * GT + i + 1) * P],
                                              xn[:, i, c * P:(c + 1) * P], ident)
                    mm.then_inc(t_xnT, 1)
                if step and step[0] == "q":
                    g = step[1]
                    take_shared()
                    for c in range(DC):
                        cs = slice(c * P, (c + 1) * P)
                        mm = three_pass(m_bank[:, c * GT * P:(c + 1) * GT * P],
                                        lambda k: wqhi[:, k, cs], lambda k: wqlo[:, k, cs],
                                        lambda k: xnThi[:, k, :], lambda k: xnTlo[:, k, :], DC)
                    mm.then_inc(t_q, 1)
                u = unit(s)
                if u is not None:
                    pe.wait_ge(a_exp, u + 1)
                    if u:
                        pe.wait_ge(a_probT, 2 * u)
                    for i in range(KC):
                        tb = t_bank[i // 3]
                        mm = pe.transpose(tb[:, (i % 3) * P:(i % 3 + 1) * P], prob[u % 2][:, i * P:(i + 1) * P], ident)
                        if i in (2, KC - 1):
                            mm.then_inc(t_probT, 1)
                step = late_step(s)
                if step:
                    what, t = step
                    take_shared()
                    if what == "wo":
                        pe.wait_ge(v_attnT, t + 1)
                        mm = three_pass(m_bank[:, 0:D], lambda k: attnThi[:, k, :], lambda k: attnTlo[:, k, :],
                                        lambda k: wohi[:, k, :], lambda k: wolo[:, k, :], DC)
                        mm.then_inc(t_wo, 1)
                    else:
                        pe.wait_ge(a_xn2T, t + 1)
                        for c in range(DC):
                            mm = pe.matmul(m_bank[:, 0:E], xn2T[:, c, :], wg_sb[:, c, :],
                                           start=(c == 0), stop=(c == DC - 1))
                        mm.then_inc(t_logit, 1)

            pe.wait_ge(v_pick, 1)
            pickf = slot_te[:, :, :].rearrange("p t e -> p (t e)")
            pe.matmul(bank[0][:, 0:NT * E], C("before"), pickf, start=True, stop=True)
            pe.matmul(bank[1][:, 0:NT * E], ones[:, :], pickf, start=True, stop=True).then_inc(t_rank, 1)
            for q in range(NC // PART):
                pe.wait_ge(v_tile, q + 1)
                for i in range(PART):
                    n = q * PART + i
                    mm = pe.matmul(bank[2 + n // NT][:, 0:2 * NJ], onehot_row[q % 2][:, i, :], onehot_tile[q % 2][:, i, :],
                                   start=(n % NT == 0), stop=(n % NT == NT - 1))
                mm.then_inc(t_list, 1)

            pe.wait_ge(v_lists, 1)
            pe.wait_ge(p_wlo, E)
            pe.wait_ge(p_w2lo, E)
            expert = [None] * NJ
            for j in range(-2, NJ):
                if 0 <= j + 1 < NJ:
                    expert[j + 1] = pe.value_load(expert_at[0:1, j + 1:j + 2], min_val=0, max_val=(E - 1) * EW)
                if 0 <= j:
                    pe.wait_ge(v_hsq, j + 1)
                    if j >= 2:
                        pe.wait_ge(v_hT, j - 1)
                    for c in range(HC):
                        mm = pe.transpose(bank[2 + j % 2][:, c * P:(c + 1) * P], hsq[:, c * P:(c + 1) * P], ident)
                    mm.then_inc(t_hT, 1)
                if j + 2 < NJ:
                    i = j + 2
                    pe.wait_ge(d_xg[i % 3], 16 * (i // 3 + 1))
                    if i >= 2:
                        pe.wait_ge(v_xgT, i - 1)
                    for c in range(DC):
                        mm = pe.transpose(bank[4 + i % 2][:, c * P:(c + 1) * P], xg[i % 3][:, c * P:(c + 1) * P], ident)
                    mm.then_inc(t_xgT, 1)
                if 0 <= j + 1 < NJ:
                    i = j + 1
                    pe.wait_ge(v_xgT, i + 1)
                    if i >= 2:
                        pe.wait_ge(v_hsq, i - 1)
                    w = lambda part, k: part[:, bass.ds(expert[i] + k * H, H)]
                    mm = three_pass(bank[i % 2][:, :], lambda k: xgThi[i % 2][:, k, :], lambda k: xgTlo[i % 2][:, k, :],
                                    lambda k: w(w1hi, k), lambda k: w(w1lo, k), DC)
                    mm.then_inc(t_h, 1)
                if 0 <= j:
                    pe.wait_ge(v_hT, j + 1)
                    if j >= 2:
                        pe.wait_ge(a_y, j - 1)
                    w = lambda part, k: part[:, bass.ds(expert[j] + k * D, D)]
                    mm = three_pass(bank[6 + j % 2][:, 0:D], lambda k: hThi[:, k, :], lambda k: hTlo[:, k, :],
                                    lambda k: w(w2hi, k), lambda k: w(w2lo, k), HC)
                    mm.then_inc(t_y, 1)

        @block.vector
        def _(dve):
            own = [0]

            def link(ins):
                own[0] += 1
                ins.then_inc(v_own, 1)
                dve.wait_ge(v_own, own[0])

            for i in range(2):
                dve.memset(prob[i][:, UC:UPAD], 0.0).then_inc(v_init, 1)
            dve.wait_ge(d_const, 16)
            dve.tensor_copy(vals[:, :, :, :, :].rearrange("p b c i (w e) -> p (b c) (i w) e", e=VW)[:, :, :, DH],
                            C("vmask").unsqueeze(1).broadcast_to([P, 2 * B, KC * WIN])).then_inc(v_vals, 1)
            for c in range(DC):
                dve.wait_ge(a_kT, c + 1)
                if c:
                    dve.wait_ge(v_klo, c)
                dve.tensor_tensor(kblock[:, :, :, :],
                                       kT[:, c, :].rearrange("p (b k) -> p b k", k=KEYS).unsqueeze(2).broadcast_to([P, B, QH, KEYS]),
                                       C("kmask").unsqueeze(1).unsqueeze(3).broadcast_to([P, B, QH, KEYS]), ALU.mult).then_inc(v_kblock, 1)
                dve.wait_ge(v_kblock, c + 1)
                dve.wait_ge(a_khi, c + 1)
                dve.tensor_tensor(klo[:, c, :, :], kblock[:, :, :, :].rearrange("p b h k -> p b (h k)"),
                                  khi[:, c, :, :].bitcast(F32), ALU.subtract).then_inc(v_klo, 1)
            for n in range(B * KC):
                b, i = divmod(n, KC)
                dve.wait_ge(t_v, n + 1)
                mask = C("vmask")[:, i * WIN:(i + 1) * WIN]
                dve.tensor_tensor(vals[:, b, :, i, :].rearrange("p c (w e) -> p c w e", e=VW)[:, :, :, 0:DH],
                                  bank[4 + n % 4][:, 0:2 * WIN * DH].rearrange("p (c w e) -> p c w e", c=2, e=DH),
                                  mask.unsqueeze(1).unsqueeze(3).broadcast_to([P, 2, WIN, DH]), ALU.mult).then_inc(v_vals, 1)
            dve.wait_ge(a_wqo, 2)
            dve.tensor_tensor(wqlo[:, :, :], wq_sb[:, :, :], wqhi[:, :, :].bitcast(F32), ALU.subtract).then_inc(v_wqo, 1)
            dve.tensor_tensor(wolo[:, :, :], wo_sb[:, :, :], wohi[:, :, :].bitcast(F32), ALU.subtract).then_inc(v_wqo, 1)

            for s in SLOTS:
                u = unit(s + 1)
                if u is not None:
                    dve.wait_ge(t_score, u + 1)
                    dve.wait_ge(v_sub, u)
                    for j in range(2):
                        src = score_bank[u % 2][j][:, 0:QC].rearrange("p (h k) -> p h k", k=KEYS)
                        ins = dve.tensor_reduce(rowmax[:, j * QH:(j + 1) * QH], src, AX.X, ALU.max)
                    link(ins)
                    if u >= 2:
                        dve.wait_ge(t_probT, 2 * (u - 1))
                    for j in range(2):
                        src = score_bank[u % 2][j][:, 0:QC].rearrange("p (h k) -> p h k", k=KEYS)
                        ins = dve.tensor_tensor(prob[u % 2][:, j * QC:(j + 1) * QC].rearrange("p (h k) -> p h k", k=KEYS), src,
                                                rowmax[:, j * QH:(j + 1) * QH].unsqueeze(2).broadcast_to([P, QH, KEYS]), ALU.subtract)
                    ins.then_inc(v_sub, 1)
                step = early_step(s)
                if step and step[0] == "attnT":
                    t = step[1]
                    dve.wait_ge(a_attnT, t + 1)
                    dve.tensor_tensor(attnTlo[:, :, :], m_bank[:, 0:D].rearrange("p (c n) -> p c n", n=P),
                                      attnThi[:, :, :].bitcast(F32), ALU.subtract).then_inc(v_attnT, 1)
                u = unit(s - 1)
                if u is not None:
                    t, c = divmod(u, 2)
                    dve.wait_ge(t_pv, u + 1)
                    if c == 0 and t:
                        dve.wait_ge(t_attnT, t)
                    pv = v_bank[:, 0:UH * VW].rearrange("p (h e) -> p h e", e=VW)
                    dve.wait_ge(v_attn, u)
                    link(dve.reciprocal(recip[:, :], pv[:, :, DH]))
                    dve.tensor_tensor(attn[:, c * P:(c + 1) * P].rearrange("p (h e) -> p h e", e=DH), pv[:, :, 0:DH],
                                      recip[:, :].unsqueeze(2).broadcast_to([P, UH, DH]), ALU.mult).then_inc(v_attn, 1)
                step = middle_step(s)
                if step and step[0] == "xnT":
                    g = step[1]
                    dve.wait_ge(a_xnT, g + 1)
                    dve.tensor_tensor(xnTlo[:, :, :].rearrange("p c n -> p (c n)"), m_bank[:, :],
                                      xnThi[:, :, :].rearrange("p c n -> p (c n)").bitcast(F32), ALU.subtract).then_inc(v_xnT, 1)
                if step and step[0] == "q":
                    g = step[1]
                    dve.wait_ge(a_q, DC * (g + 1))
                    for c in range(DC):
                        ins = dve.scalar_tensor_tensor(out=qTlo[g % 2][:, c, :], in0=m_bank[:, c * GT * P:(c + 1) * GT * P],
                                                       scalar=bq_sb[:, c:c + 1], in1=qThi[g % 2][:, c, :].bitcast(F32),
                                                       op0=ALU.add, op1=ALU.subtract)
                    ins.then_inc(v_q, 1)
                g = norm1_stats(s)
                if g is not None:
                    dve.wait_ge(d_x[g % XBUF], 16 * (g // XBUF + 1))
                    dve.wait_ge(v_var1, g)
                    dve.wait_ge(v_xn, g)
                    dve.wait_ge(p_rs1, g)
                    for i in range(GT):
                        ins = dve.bn_stats(st1[:, i, :], xs[g % XBUF][:, i, :])
                    link(ins)
                    for i in range(GT):
                        ins = dve.bn_aggr(mv1[:, i, :], st1[:, i, :])
                    link(ins)
                    dve.tensor_scalar(ve1[:, :], mv1[:, :, 1], EPS, None, ALU.add).then_inc(v_var1, 1)
                g = norm1_apply(s)
                if g is not None:
                    dve.wait_ge(p_rs1, g + 1)
                    if g:
                        dve.wait_ge(t_xnT, g)
                    for i in range(GT):
                        ins = dve.tensor_scalar(xn[:, i, :], xs[g % XBUF][:, i, :], mv1[:, i, 0:1], rs1[:, i:i + 1],
                                                ALU.subtract, ALU.mult)
                    ins.then_inc(v_xn, 1)
                t = norm2_apply(s)
                if t is not None:
                    dve.wait_ge(p_rs2, t + 1)
                    if t >= 2:
                        dve.wait_ge(d_xn2[t % 2], 16 * (t // 2))
                        dve.wait_ge(t_xn2T, t - 1)
                    dve.tensor_scalar(xn2[t % 2][:, :], xs[t // GT % XBUF][:, t % GT, :], mv2[:, 0:1], rs2[:, 0:1],
                                      ALU.subtract, ALU.mult).then_inc(v_xn2, 1)
                step = late_step(s)
                if step and step[0] == "wo":
                    t = step[1]
                    x1 = xs[t // GT % XBUF][:, t % GT, :]
                    dve.wait_ge(t_wo, t + 1)
                    dve.wait_ge(p_xb, t // GT + 1)
                    dve.scalar_tensor_tensor(out=x1, in0=m_bank[:, 0:D], scalar=tg[:, 0:1], in1=x1,
                                             op0=ALU.mult, op1=ALU.add).then_inc(v_x1, 1)
                    dve.wait_ge(v_x1, t + 1)
                    dve.wait_ge(v_xn2, t)
                    link(dve.bn_stats(st2[:, :], x1))
                    link(dve.bn_aggr(mv2[:, :], st2[:, :]))
                    dve.tensor_scalar(ve2[:, :], mv2[:, 1:2], EPS, None, ALU.add).then_inc(v_var2, 1)
                if step and step[0] == "logit":
                    t = step[1]
                    dve.wait_ge(t_logit, t + 1)
                    dve.tensor_copy(logits[:, t, :], m_bank[:, 0:E]).then_inc(v_logit, 1)

            TE = [P, NT, E]
            over_e = lambda a: a.unsqueeze(2).broadcast_to(TE)
            over_t = lambda a: a.unsqueeze(1).broadcast_to(TE)
            tt = lambda *a: link(dve.tensor_tensor(*a))
            ts = lambda *a: link(dve.tensor_scalar(*a))
            dve.wait_ge(v_logit, NT)
            dve.wait_ge(p_wlo, E)
            for i in range(2):
                dve.wait_ge(d_xn2[i], 16 * (NT // 2))
            for i in range(XBUF):
                dve.wait_ge(d_x1[i], 16 * GT * (NG // XBUF))
            best, second, key, tmp = top[:, 0, :], top[:, 1, :], small[:, 0, :], small[:, 1, :]

            def choose(values, best_of, chosen):
                link(dve.tensor_reduce(best_of, values, AX.X, ALU.max))
                tt(chosen, values, over_e(best_of), ALU.is_equal)
                tt(chosen, chosen, over_t(C("lowest")), ALU.mult)
                link(dve.tensor_reduce(key, chosen, AX.X, ALU.max))
                tt(chosen, chosen, over_e(key), ALU.is_equal)

            choose(logits[:, :, :], best, pick[0][:, :, :])
            dve.tensor_tensor(lgm[:, :, :], logits[:, :, :], over_e(best), ALU.subtract).then_inc(v_lgm, 1)
            dve.wait_ge(v_lgm, 1)
            link(dve.tensor_reduce(tmp, lgm[:, :, :], AX.X, ALU.min))
            ts(tmp, tmp, 2.0, -1.0, ALU.mult, ALU.add)
            tt(count[0][:, :, :], pick[0][:, :, :], over_e(tmp), ALU.mult)
            tt(count[0][:, :, :], count[0][:, :, :], lgm[:, :, :], ALU.add)
            choose(count[0][:, :, :], second, pick[1][:, :, :])
            dve.tensor_tensor(slot_te[:, :, :], pick[0][:, :, :], pick[1][:, :, :], ALU.add).then_inc(v_pick, 1)
            dve.wait_ge(a_prob8, 1)
            link(dve.tensor_reduce(small[:, 2, :], prob8[:, :, :], AX.X, ALU.add))
            link(dve.reciprocal(small[:, 2, :], small[:, 2, :]))
            tt(prob8[:, :, :], prob8[:, :, :], over_e(small[:, 2, :]), ALU.mult)
            for k in range(CHOICES):
                tt(count[1][:, :, :], prob8[:, :, :], pick[k][:, :, :], ALU.mult)
                link(dve.tensor_reduce(tile_w[:, k, :], count[1][:, :, :], AX.X, ALU.add))
            tt(small[:, 3, :], tile_w[:, 0, :], tile_w[:, 1, :], ALU.add)
            ts(small[:, 3, :], small[:, 3, :], 1e-8, None, ALU.add)
            link(dve.reciprocal(small[:, 3, :], small[:, 3, :]))
            tt(tile_w[:, :, :], tile_w[:, :, :], small[:, 3, :].unsqueeze(1).broadcast_to([P, CHOICES, NT]), ALU.mult)
            ts(tile_w[:, :, :], tile_w[:, :, :], tg[:, 1:2], None, ALU.mult)
            dve.wait_ge(t_rank, 1)
            of_tile = totals[:, :, :]
            link(dve.tensor_copy(of_tile.rearrange("p t e -> p (t e)"), bank[1][:, 0:NT * E]))
            link(dve.tensor_copy(count[0][:, :, :], of_tile))
            src, dst = count
            step = 1
            while step < NT:
                link(dve.tensor_copy(dst[:, 0:step, :], src[:, 0:step, :]))
                tt(dst[:, step:, :], src[:, step:, :], src[:, :NT - step, :], ALU.add)
                src, dst = dst, src
                step *= 2
            tt(dst[:, :, :], over_t(src[:, NT - 1, :]), over_e(C("full")), ALU.is_gt)
            link(dve.tensor_reduce(need[:, :], dst[:, :, :].rearrange("p t e -> p e t"), AX.X, ALU.add))
            link(dve.tensor_copy(first[0][:, :], need[:, :]))
            f, f2 = first
            step = 1
            while step < E:
                link(dve.tensor_copy(f2[:, 0:step], f[:, 0:step]))
                tt(f2[:, step:], f[:, step:], f[:, :E - step], ALU.add)
                f, f2 = f2, f
                step *= 2
            tt(ended[:, :, :], f[0:1, 0:E - 1].unsqueeze(1).broadcast_to([1, NJ, E - 1]),
               C("iota")[0:1, 0:NJ].unsqueeze(2).broadcast_to([1, NJ, E - 1]), ALU.is_le)
            link(dve.tensor_reduce(listf[0:1, 0, :], ended[:, :, :], AX.X, ALU.add))
            ts(expert_at[:, :], listf[0:1, 0, :], float(EW), None, ALU.mult)
            tt(f2[:, :], f[:, :], need[:, :], ALU.subtract)
            ts(base[:, :], f2[:, :], float(P), None, ALU.mult)
            tt(src[:, :, :], src[:, :, :], of_tile, ALU.subtract)
            tt(src[:, :, :], src[:, :, :], over_t(base[:, :]), ALU.add)
            tt(src[:, :, :], src[:, :, :], bank[0][:, 0:NT * E].rearrange("p (t e) -> p t e", e=E), ALU.add)
            for k in range(CHOICES):
                tt(dst[:, :, :], src[:, :, :], pick[k][:, :, :], ALU.mult)
                link(dve.tensor_reduce(slot[:, k, :], dst[:, :, :], AX.X, ALU.add))
            link(dve.tensor_copy(slot_i[:, :], slot[:, :, :].rearrange("p k t -> p (k t)")))
            ts(srow_i[:, :], slot_i[:, :], P - 1, None, ALU.bitwise_and)
            ts(stile_i[:, :], slot_i[:, :], P.bit_length() - 1, None, ALU.logical_shift_right)
            link(dve.tensor_copy(srow[:, :], srow_i[:, :]))
            link(dve.tensor_copy(stile[:, :], stile_i[:, :]))
            for q in range(NC // PART):
                ns = slice(q * PART, (q + 1) * PART)
                if q >= 2:
                    dve.wait_ge(t_list, q - 1)
                dve.tensor_tensor(onehot_row[q % 2][:, :, :], srow[:, ns].unsqueeze(2).broadcast_to([P, PART, P]),
                                  C("iota").unsqueeze(1).broadcast_to([P, PART, P]), ALU.is_equal)
                hit = onehot_tile[q % 2][:, :, NJ:2 * NJ]
                tt(hit, stile[:, ns].unsqueeze(2).broadcast_to([P, PART, NJ]),
                   C("iota")[:, 0:NJ].unsqueeze(1).broadcast_to([P, PART, NJ]), ALU.is_equal)
                t0 = q * PART % NT
                dve.tensor_tensor(onehot_tile[q % 2][:, :, 0:NJ], hit.bitcast(F32),
                                  C("token")[:, t0:t0 + PART].unsqueeze(2).broadcast_to([P, PART, NJ]),
                                  ALU.mult).then_inc(v_tile, 1)
            dve.wait_ge(t_list, NC // PART)
            link(dve.tensor_copy(listed[:, :], bank[2][:, 0:2 * NJ]))
            tok, filled, row = listf[:, 0, :], listf[:, 1, :], listf[:, 2, :]
            tt(tok, listed[:, 0:NJ], bank[3][:, 0:NJ], ALU.add)
            tt(filled, listed[:, NJ:2 * NJ], bank[3][:, NJ:2 * NJ], ALU.add)
            link(dve.scalar_tensor_tensor(out=row, in0=tok, scalar=2.0, in1=bank[3][:, NJ:2 * NJ], op0=ALU.mult, op1=ALU.add))
            ts(filled, filled, -1.0, 1.0, ALU.mult, ALU.add)
            tt(filled, filled, C("spare"), ALU.mult)
            tt(row, row, filled, ALU.add)
            link(dve.tensor_copy(gather_at[:, :], tok))
            dve.tensor_copy(scatter_at[:, :], row).then_inc(v_lists, 1)

            for j in range(-2, NJ):
                if 0 <= j:
                    dve.wait_ge(a_hT, j + 1)
                    dve.tensor_tensor(hTlo[:, :, :].rearrange("p c n -> p (c n)"), bank[2 + j % 2][:, :],
                                      hThi[:, :, :].rearrange("p c n -> p (c n)").bitcast(F32), ALU.subtract).then_inc(v_hT, 1)
                if j + 2 < NJ:
                    i = j + 2
                    dve.wait_ge(a_xgT, i + 1)
                    dve.tensor_tensor(xgTlo[i % 2][:, :, :].rearrange("p c n -> p (c n)"), bank[4 + i % 2][:, 0:D],
                                      xgThi[i % 2][:, :, :].rearrange("p c n -> p (c n)").bitcast(F32),
                                      ALU.subtract).then_inc(v_xgT, 1)
                if 0 <= j + 1 < NJ:
                    i = j + 1
                    dve.wait_ge(a_relu, i + 1)
                    dve.wait_ge(t_hT, i)
                    dve.tensor_tensor(hsq[:, :], bank[i % 2][:, :], hrelu[:, :], ALU.mult).then_inc(v_hsq, 1)

            dve.wait_ge(d_x1all, 16)
            for c in range(NT // CT):
                dve.wait_ge(d_yin[c % 3], 16 * (c // 3 + 1))
                for k in range(CHOICES):
                    for i in range(CT):
                        t = c * CT + i
                        ins = dve.scalar_tensor_tensor(out=x1_all[:, t, :], in0=y_in[c % 3][:, i, k, :],
                                                       scalar=tile_w[:, k, t:t + 1], in1=x1_all[:, t, :],
                                                       op0=ALU.mult, op1=ALU.add)
                    if k < CHOICES - 1:
                        link(ins)
                ins.then_inc(v_out, 1)


_INS = ["x", "ctx_1024", "g_xattn", "g_ffn", "L0_xattn_Wq", "L0_xattn_Wk", "L0_xattn_Wv", "L0_xattn_Wo",
        "L0_xattn_bq", "L0_xattn_bk", "L0_xattn_bv", "L0_xattn_bo", "L0_ffn_Wg", "L0_ffn_W1", "L0_ffn_W2"]


def kernel(**inputs):
    import numpy as _np
    import concourse.bacc as _bacc
    from concourse import mybir as _mybir
    from concourse.bass_utils import run_bass_kernel_spmd as _run

    nc = _bacc.Bacc("TRN2", target_bir_lowering=False, num_devices=1)
    arrays, args = {}, []
    for name in _INS:
        a = _np.ascontiguousarray(inputs[name])
        arrays[f"in_{name}"] = a
        args.append(nc.dram_tensor(f"in_{name}", a.shape, _mybir.dt.from_np(a.dtype), kind="ExternalInput").ap())
    table = constants()[0]
    arrays["in_constants"] = table
    args.append(nc.dram_tensor("in_constants", table.shape, _mybir.dt.float32, kind="ExternalInput").ap())
    args.append(nc.dram_tensor("out", (B, S, D), _mybir.dt.float32, kind="ExternalOutput").ap())
    build(nc, *args)
    r = _run(nc, [arrays], core_ids=[0])
    return r.results[0]["out"]
```

```python
from contextlib import ExitStack

import numpy as np
import concourse.bass as bass
from concourse import mybir

F32 = mybir.dt.float32
F32R = mybir.dt.float32r
I32 = mybir.dt.int32
ALU = mybir.AluOpType
ACT = mybir.ActivationFunctionType
AX = mybir.AxisListType

P = 128
B, S, D = 4, 1024, 256
KEYS = 77
HEADS, DH = 16, 16
E, H = 8, 512
EPS = 1e-5

N = B * S
NT = N // P
DC = D // P
HC = H // P
UNITS = 2 * NT
UH = HEADS // 2
UC = UH * KEYS
QH = UH // 2
QC = QH * KEYS
KC = -(-UC // P)
UPAD = KC * P
WIN = 3
VW = DH + 1
HEAD0 = [min(P * i // KEYS, UH - WIN) for i in range(KC)]
GT = 2
NG = NT // GT
GPB = NG // B
CHOICES = 2
NJ = (CHOICES * N + E * (P - 1)) // P
NC = NT * CHOICES
XBUF = 5
XG = 9
HW = 512


def constants():
    p = np.arange(P)[:, None]
    row = np.arange(P)[None, :]
    head = [(P * i + p) // KEYS for i in range(KC)]
    parts = {
        "ident": p == row,
        "before": p < row,
        "kmask": p // DH == np.arange(UH)[None, :],
        "vmask": np.concatenate([head[i] == HEAD0[i] + np.arange(WIN)[None, :] for i in range(KC)], 1),
        "iota": row + 0 * p,
        "token": P * np.arange(NT)[None, :] + p,
        "spare": CHOICES * N + P * np.arange(NJ)[None, :] + p,
        "lowest": E - np.arange(E)[None, :] + 0 * p,
        "full": P * np.arange(NT)[None, :] + 0 * p,
    }
    at, cols = {}, 0
    for name, a in parts.items():
        at[name] = (cols, cols + a.shape[1])
        cols += a.shape[1]
    return np.concatenate([a.astype(np.float32) for a in parts.values()], 1), at


def build(nc, x, ctx_in, g_xattn, g_ffn, wq, wk, wv, wo, bq, bk, bv, bo, wg, w1, w2, consts, out):
    _, at = constants()
    x1_dram = nc.dram_tensor("x1_scratch", (N, D), F32).ap()
    xn2_dram = nc.dram_tensor("xn2_scratch", (N, D), F32).ap()
    y_dram = nc.dram_tensor("y_scratch", (CHOICES * N + NJ * P, D), F32).ap()

    rows = lambda a: a.rearrange("(t p) d -> p t d", p=P)
    x_rows = rows(x.rearrange("b s d -> (b s) d"))
    out_rows = rows(out.rearrange("b s d -> (b s) d"))
    x1_rows = rows(x1_dram)
    y_rows = y_dram[0:CHOICES * N, :].rearrange("(t p k) d -> p t k d", p=P, k=CHOICES)

    ctx = ExitStack()
    with ctx:
        def sem(name):
            return ctx.enter_context(nc.semaphore(name))

        def place(stack, name, shape, dt=F32):
            return stack.enter_context(nc.sbuf_tensor(name, shape, dt))

        cst = place(ctx, "cst", [P, consts.shape[1]])
        C = lambda name: cst[:, at[name][0]:at[name][1]]
        ident = C("ident")
        ones = place(ctx, "ones", [P, P])
        logits = place(ctx, "logits", [P, NT, E])
        gates = place(ctx, "gates", [P, 2])
        tg = place(ctx, "tg", [P, 2])
        w1hi = place(ctx, "w1hi", [P, E * DC * H], F32R)
        w1lo = place(ctx, "w1lo", [P, E * DC * H], F32R)
        EW = DC * H
        with ExitStack() as early:
            ctx_sb = place(early, "ctx_sb", [KEYS, B, D])
            ctxT = place(early, "ctxT", [P, DC, B, 3 * KEYS])
            wk_sb = place(early, "wk_sb", [P, DC, D])
            wv_sb = place(early, "wv_sb", [P, DC, D])
            wq_sb = place(early, "wq_sb", [P, DC, D])
            bv_sb = place(early, "bv_sb", [P, DC])
            bv_wide = place(early, "bv_wide", [P, DC, P])
            wo_sb = place(early, "wo_sb", [P, DC, D])
        w2hi = place(ctx, "w2hi", [P, E * HC * D], F32R)
        tile_w = place(ctx, "tile_w", [P, CHOICES, NT])
        gather_at = place(ctx, "gather_at", [P, NJ], I32)
        scatter_at = place(ctx, "scatter_at", [P, NJ], I32)
        expert_at = place(ctx, "expert_at", [1, NJ], I32)

        with ExitStack() as a:
            kT = place(a, "kT", [P, DC, B * KEYS])
            kblock = place(a, "kblock", [P, UH, KEYS])
            khi = [place(a, f"khi{i}", [P, DC, UC], F32R) for i in range(2)]
            klo = [place(a, f"klo{i}", [P, DC, UC], F32R) for i in range(2)]
            vals = place(a, "vals", [P, B, 2, KC, UH * VW])
            wqhi = place(a, "wqhi", [P, DC, D], F32R)
            wqlo = place(a, "wqlo", [P, DC, D], F32R)
            wohi = place(a, "wohi", [P, DC, D], F32R)
            wolo = place(a, "wolo", [P, DC, D], F32R)
            wg_sb = place(a, "wg_sb", [P, DC, E])
            bo_sb = place(a, "bo_sb", [P, D])
            bq_sb = place(a, "bq_sb", [P, DC])
            bk_sb = place(a, "bk_sb", [P, DC])
            raw = [place(a, f"raw{i}", [P, EW]) for i in range(2)]
            xs = [place(a, f"xs{i}", [P, GT, D]) for i in range(XBUF)]
            xn = place(a, "xn", [P, GT, D])
            xnT = place(a, "xnT", [P, DC, GT * P])
            qT = place(a, "qT", [P, DC, GT * P])
            xnThi = place(a, "xnThi", [P, DC, GT * P], F32R)
            xnTlo = place(a, "xnTlo", [P, DC, GT * P], F32R)
            qThi = [place(a, f"qThi{i}", [P, DC, GT * P], F32R) for i in range(2)]
            qTlo = [place(a, f"qTlo{i}", [P, DC, GT * P], F32R) for i in range(2)]
            prob = [place(a, f"prob{i}", [P, UPAD]) for i in range(2)]
            probT = [place(a, f"probT{i}", [P, KC, P]) for i in range(2)]
            attn = place(a, "attn", [P, D])
            attnThi = place(a, "attnThi", [P, DC, P], F32R)
            attnTlo = place(a, "attnTlo", [P, DC, P], F32R)
            xn2 = [place(a, f"xn2{i}", [P, D]) for i in range(2)]
            xn2T = place(a, "xn2T", [P, DC, P])
            rowmax = place(a, "rowmax", [P, UH])
            recip = place(a, "recip", [P, UH])
            st1 = place(a, "st1", [P, GT, 6])
            mv1 = place(a, "mv1", [P, GT, 2])
            ve1 = place(a, "ve1", [P, GT])
            rs1 = place(a, "rs1", [P, GT])
            nm1 = place(a, "nm1", [P, GT])
            nr1 = place(a, "nr1", [P, GT])
            st2 = place(a, "st2", [P, 6])
            mv2 = place(a, "mv2", [P, 2])
            ve2 = place(a, "ve2", [P, 1])
            rs2 = place(a, "rs2", [P, 1])
            nm2 = place(a, "nm2", [P, 1])
            nr2 = place(a, "nr2", [P, 1])
            half = place(a, "half", [P, GT])
        w2lo = place(ctx, "w2lo", [P, E * HC * D], F32R)
        with ExitStack() as r:
            raw2 = [place(r, f"raw2{i}", [P, EW]) for i in range(2)]
            PART = NT // 2
            onehot_row = [place(r, f"onehot_row{i}", [P, PART, P], F32R) for i in range(2)]
            onehot_tile = [place(r, f"onehot_tile{i}", [P, PART, 2 * NJ], F32R) for i in range(2)]
            ended = place(r, "ended", [1, NJ, E - 1])
            TE = [P, NT, E]
            lgm = place(r, "lgm", TE)
            prob8 = place(r, "prob8", TE)
            pick = [place(r, f"pick{i}", TE) for i in range(CHOICES)]
            count = [place(r, f"count{i}", TE) for i in range(2)]
            slot_te = place(r, "slot_te", TE)
            totals = lgm
            top = place(r, "top", [P, CHOICES, NT])
            small = place(r, "small", [P, 4, NT])
            slot = place(r, "slot", [P, CHOICES, NT])
            slot_i = place(r, "slot_i", [P, NC], I32)
            srow_i = place(r, "srow_i", [P, NC], I32)
            stile_i = place(r, "stile_i", [P, NC], I32)
            srow = place(r, "srow", [P, NC])
            stile = place(r, "stile", [P, NC])
            need = place(r, "need", [P, E])
            first = [place(r, f"first{i}", [P, E]) for i in range(2)]
            base = place(r, "base", [P, E])
            listed = place(r, "listed", [P, 2 * NJ])
            listf = place(r, "listf", [P, 3, NJ])
        with ExitStack() as m:
            x1_all = place(m, "x1_all", [P, NT, D])
            xg = [place(m, f"xg{i}", [P, D]) for i in range(XG)]
            xgThi = [place(m, f"xgThi{i}", [P, DC, P], F32R) for i in range(2)]
            xgTlo = [place(m, f"xgTlo{i}", [P, DC, P], F32R) for i in range(2)]
            hrelu = place(m, "hrelu", [P, H])
            hsq = [place(m, f"hsq{i}", [P, H]) for i in range(2)]
            hThi = [place(m, f"hThi{i}", [P, HC, P], F32R) for i in range(2)]
            hTlo = [place(m, f"hTlo{i}", [P, HC, P], F32R) for i in range(2)]
            y_sb = [place(m, f"y_sb{i}", [P, D]) for i in range(2)]
            CT = 4
        YW = CT * CHOICES * D
        y_in = [w[:, i * YW:(i + 1) * YW].bitcast(F32).rearrange("p (t k d) -> p t k d", k=CHOICES, d=D)
                for w in (w1hi, w1lo) for i in range(E * EW // YW)]

        pair = [ctx.enter_context(nc.psum_tensor(f"pair{i}", [P, 2, HW], F32)) for i in range(4)]
        bank = [pair[i // 2][:, i % 2, :] for i in range(8)]
        t_bank = [bank[4], bank[5]]
        v_bank = bank[5][:, 2 * P:]
        shared_bank = [bank[6], bank[7]]

        d_const, d_ctx, d_wk, d_wv, d_wq, d_wo, d_bk, d_bq, d_bv, d_bo, d_gate = (
            sem("d_" + n) for n in ("const", "ctx", "wk", "wv", "wq", "wo", "bk", "bq", "bv", "bo", "gate"))
        d_x = [sem(f"d_x{i}") for i in range(XBUF)]
        d_x1 = [sem(f"d_x1{i}") for i in range(XBUF)]
        d_xn2 = [sem(f"d_xn2{i}") for i in range(2)]
        d_raw = [sem(f"d_raw{i}") for i in range(2)]
        d_raw2 = [sem(f"d_raw2{i}") for i in range(2)]
        p_w2lo, a_w2hi = sem("p_w2lo"), sem("a_w2hi")
        p_init, p_xb, p_wlo = (sem("p_" + n) for n in ("init", "xb", "wlo"))
        p_kblock, p_klo, p_wqo, v_bo, v_bvw, v_ctxT, t_bo, a_wq, a_wo = (
            sem(n) for n in ("p_kblock", "p_klo", "p_wqo", "v_bo", "v_bvw", "v_ctxT", "t_bo", "a_wq", "a_wo"))
        p_own, p_nr1, p_nr2, p_xnT, p_q = (sem("p_" + n) for n in ("own", "nr1", "nr2", "xnT", "q"))
        a_xn, a_xn2, a_xnTf, a_qf = (sem("a_" + n) for n in ("xn", "xn2", "xnTf", "qf"))
        v_bn1, v_bn2, v_max, v_recip, v_ones = (sem("v_" + n) for n in ("bn1", "bn2", "max", "recip", "ones"))
        t_ctx, t_k, t_v = (sem("t_" + n) for n in ("ctx", "k", "v"))
        t_xnT, t_q, t_score, t_probT, t_pv, t_attnT, t_wo, t_xn2T, t_logit = (
            sem("t_" + n) for n in ("xnT", "q", "score", "probT", "pv", "attnT", "wo", "xn2T", "logit"))
        a_tanh, a_ctxT, a_kT, a_khi = (sem("a_" + n) for n in ("tanh", "ctxT", "kT", "khi"))
        a_xnT, a_q, a_exp, a_probT, a_attnT, a_xn2T, a_whi = (
            sem("a_" + n) for n in ("xnT", "q", "exp", "probT", "attnT", "xn2T", "whi"))
        v_init, v_kblock, v_klo, v_vals, v_var1, v_sub, v_attn, v_attnT = (
            sem("v_" + n) for n in ("init", "kblock", "klo", "vals", "var1", "sub", "attn", "attnT"))
        v_x1, v_var2, v_logit, v_own = (sem("v_" + n) for n in ("x1", "var2", "logit", "own"))
        a_own, a_prob8 = sem("a_own"), sem("a_prob8")
        v_lgm, v_pick, v_row, v_tile, v_lists = (sem("v_" + n) for n in ("lgm", "pick", "row", "tile", "lists"))
        t_rank, t_list = sem("t_rank"), sem("t_list")
        d_x1all = sem("d_x1all")
        d_xg = [sem(f"d_xg{i}") for i in range(XG)]
        d_ys = [sem(f"d_ys{i}") for i in range(2)]
        d_yin = [sem(f"d_yin{i}") for i in range(NT // CT)]
        d_out = sem("d_out")
        t_xgT, t_h, t_hT, t_y = (sem("t_" + n) for n in ("xgT", "h", "hT", "y"))
        a_xgT, a_relu, a_hT, a_y = (sem("a_" + n) for n in ("xgT", "relu", "hT", "y"))
        v_xgT, v_hsq, v_hT, v_out = (sem("v_" + n) for n in ("xgT", "hsq", "hT", "out"))

        SLOTS = range(-9, UNITS + 7)

        UB = UNITS // B

        def tile_at(s, lag):
            t, odd = divmod(s - lag, 2)
            return t if not odd and 0 <= t < NT else None

        def group_at(s, lead):
            g, off = divmod(s + lead, 2 * GT)
            return g if not off and 0 <= g < NG else None

        attnT_tile = lambda s: tile_at(s, 3)
        wo_tile = lambda s: tile_at(s, 4)
        norm2_stats = lambda s: tile_at(s, 5)
        norm2_apply = lambda s: tile_at(s, 6)
        xn2T_tile = lambda s: tile_at(s, 7)
        logit_tile = lambda s: tile_at(s, 8)
        norm1_stats = lambda s: group_at(s, 9)
        norm1_apply = lambda s: group_at(s, 8)
        xnT_group = lambda s: group_at(s, 7)
        q_group = lambda s: group_at(s, 5)

        def value_step(s):
            for b in range(B):
                at_slots = [-9, -6, -5, -2, -1] if b == 0 else [UB * b - k for k in (10, 7, 6, 3, 2)]
                if s in at_slots:
                    return b * KC + at_slots.index(s)

        def key_step(s):
            for b in range(B):
                for c in range(DC):
                    if s == (c - 5 if b == 0 else UB * b - 12 + 4 * c):
                        return b, c

        def key_split(s):
            step = key_step(s)
            if step and step[0] == 0:
                return step
            step = key_step(s - 1)
            return step if step and step[0] else None

        def weight_piece(s):
            return s // 8 if s % 8 == 2 and 0 <= s // 8 < E else None

        def unit(u):
            return u if 0 <= u < UNITS else None

        def shared_steps(s):
            steps = (("xn2T", xn2T_tile(s)), ("logit", logit_tile(s)), ("attnT", attnT_tile(s)), ("wo", wo_tile(s)),
                     ("xnT", xnT_group(s)), ("q", q_group(s)), ("value", value_step(s)))
            return [step for step in steps if step[1] is not None]

        shared_order = [step for s in SLOTS for step in shared_steps(s)]
        shared_place = {step: shared_bank[n % 2] for n, step in enumerate(shared_order)}
        drained_by = {"xnT": a_xnTf, "q": a_qf, "attnT": v_attnT, "wo": v_x1, "xn2T": a_xn2T, "logit": v_logit, "value": v_vals}
        x1_stores = [GT * len(range(i, NG, XBUF)) for i in range(XBUF)]

        def part_of(w, e):
            return w[:, e * EW:(e + 1) * EW]

        def key_block(b, c):
            return (kT[:, c, b * KEYS:(b + 1) * KEYS].unsqueeze(1).broadcast_to([P, UH, KEYS]),
                    C("kmask").unsqueeze(2).broadcast_to([P, UH, KEYS]))

        def ctx_copies(c):
            return (ctxT[:, c, :, :].rearrange("p b (r k) -> p b r k", k=KEYS),
                    bank[c][:, 0:B * KEYS].rearrange("p (b k) -> p b k", k=KEYS).unsqueeze(2).broadcast_to([P, B, 3, KEYS]))

        block = ctx.enter_context(nc.Block())

        @block.sync
        def _(sp):
            sp.dma_start(cst[:, :], consts).then_inc(d_const, 16)
            sp.dma_start(wk_sb[:, :, :], wk.rearrange("(c p) n -> p c n", p=P)).then_inc(d_wk, 16)
            def load_x(g):
                if g >= XBUF:
                    sp.wait_ge(d_x1[g % XBUF], 16 * GT * (g // XBUF))
                    sp.wait_ge(a_xn2, GT * (g - XBUF + 1))
                sp.dma_start(xs[g % XBUF][:, :, :], x_rows[:, GT * g:GT * g + GT, :]).then_inc(d_x[g % XBUF], 16)

            load_x(0)
            sp.dma_start(wq_sb[:, :, :], wq.rearrange("(c p) n -> p c n", p=P)).then_inc(d_wq, 16)
            load_x(1)
            sp.dma_start(wo_sb[:, :, :], wo.rearrange("(c p) n -> p c n", p=P)).then_inc(d_wo, 16)
            sp.dma_start(wg_sb[:, :, :], wg.rearrange("(c p) n -> p c n", p=P)).then_inc(d_wo, 16)
            for g in range(2, XBUF):
                load_x(g)

            def load_w1(k):
                if k >= 2:
                    sp.wait_ge(p_wlo, k - 1)
                sp.dma_start(raw[k % 2][:, :].rearrange("p (c n) -> p c n", c=DC),
                             w1[k].rearrange("(c p) n -> p c n", p=P)).then_inc(d_raw[k % 2], 16)

            load_w1(0)
            load_w1(1)
            for s in SLOTS:
                k = weight_piece(s - 2)
                if k is not None and k + 2 < E:
                    load_w1(k + 2)
                t = wo_tile(s)
                if t is not None:
                    sp.wait_ge(v_x1, t + 1)
                    sp.dma_start(x1_rows[:, t, :], xs[t // GT % XBUF][:, t % GT, :]).then_inc(d_x1[t // GT % XBUF], 16)
                t = norm2_apply(s)
                if t is not None:
                    sp.wait_ge(a_xn2, t + 1)
                    sp.dma_start(xn2_dram[t * P:(t + 1) * P, :], xn2[t % 2][:, :]).then_inc(d_xn2[t % 2], 16)
                    if t % GT == GT - 1 and t // GT + XBUF < NG:
                        load_x(t // GT + XBUF)
            sp.wait_ge(v_logit, NT)
            sp.wait_ge(p_wlo, E)
            for i in range(2):
                sp.wait_ge(d_xn2[i], 16 * (NT // 2))
            for i in range(XBUF):
                sp.wait_ge(d_x1[i], 16 * x1_stores[i])
            for k in range(E):
                if k >= 2:
                    sp.wait_ge(p_w2lo, k - 1)
                sp.dma_start(raw2[k % 2][:, :].rearrange("p (c n) -> p c n", c=HC),
                             w2[k].rearrange("(c p) n -> p c n", p=P)).then_inc(d_raw2[k % 2], 16)
            sp.wait_ge(p_w2lo, E)
            sp.wait_ge(v_lists, 1)
            sp.dma_start(x1_all[:, :, :], x1_rows).then_inc(d_x1all, 16)
            for i in range(2):
                sp.wait_ge(d_ys[i], 16 * len(range(i, NJ, 2)))
            for c in range(NT // CT):
                sp.dma_start(y_in[c], y_rows[:, c * CT:(c + 1) * CT, :, :]).then_inc(d_yin[c], 16)
            for c in range(NT // CT):
                sp.wait_ge(v_out, c + 1)
                sp.dma_start(out_rows[:, c * CT:(c + 1) * CT, :], x1_all[:, c * CT:(c + 1) * CT, :]).then_inc(d_out, 16)
            sp.wait_ge(d_out, 16 * (NT // CT))

        @block.gpsimd
        def _(pool):
            pool.memset(ones[:, :], 1.0).then_inc(p_init, 1)
            pool.memset(half[:, :], -0.5).then_inc(p_init, 1)
            pool.memset(vals[:, :, :, :, :], 0.0).then_inc(p_init, 1)
            for c in range(DC):
                pool.dma_start(bk_sb[:, c:c + 1], bk[c * P:(c + 1) * P].unsqueeze(1)).then_inc(d_bk, 16)
            for c in range(DC):
                pool.dma_start(bq_sb[:, c:c + 1], bq[c * P:(c + 1) * P].unsqueeze(1)).then_inc(d_bq, 16)
            for c in range(DC):
                pool.dma_start(bv_sb[:, c:c + 1], bv[c * P:(c + 1) * P].unsqueeze(1)).then_inc(d_bv, 16)
            pool.dma_start(bo_sb[:, :], bo.partition_broadcast(P)).then_inc(d_bo, 16)
            pool.wait_ge(a_wq, 1)
            pool.tensor_tensor(wqlo[:, :, :], wq_sb[:, :, :], wqhi[:, :, :].bitcast(F32), ALU.subtract).then_inc(p_wqo, 1)
            pool.wait_ge(a_wo, 1)
            pool.tensor_tensor(wolo[:, :, :], wo_sb[:, :, :], wohi[:, :, :].bitcast(F32), ALU.subtract).then_inc(p_wqo, 1)
            pool.wait_ge(p_init, 2)
            own = [0]

            def link(ins):
                own[0] += 1
                ins.then_inc(p_own, 1)
                pool.wait_ge(p_own, own[0])

            def scales(mv, ve, rs, nm, nr, done):
                pool.tensor_scalar(nm, mv[:, :, 0], -1.0, None, ALU.mult)
                link(pool.tensor_scalar(ve, mv[:, :, 1], EPS, None, ALU.add))
                link(pool.tensor_tensor(rs, ve, half[:, 0:ve.shape[1]], ALU.pow))
                pool.tensor_tensor(nr, nm, rs, ALU.mult).then_inc(done, 1)

            for s in SLOTS:
                t = norm2_stats(s)
                if t is not None:
                    pool.wait_ge(v_var2, t + 1)
                    pool.wait_ge(a_xn2, t)
                    scales(mv2[:, :].unsqueeze(1), ve2[:, :], rs2[:, :], nm2[:, :], nr2[:, :], p_nr2)
                g = norm1_stats(s)
                if g is not None:
                    pool.wait_ge(v_var1, g + 1)
                    pool.wait_ge(a_xn, g)
                    scales(mv1[:, :, :], ve1[:, :], rs1[:, :], nm1[:, :], nr1[:, :], p_nr1)
                g = norm1_apply(s)
                if g is not None:
                    pool.wait_ge(a_xn, g + 1)
                    pool.wait_ge(v_bo, 1)
                    bo_b = bo_sb[:, :].unsqueeze(1).broadcast_to([P, GT, D])
                    pool.tensor_tensor(xs[g % XBUF][:, :, :], xs[g % XBUF][:, :, :], bo_b, ALU.add).then_inc(p_xb, 1)
                step = key_split(s)
                if step and step[0]:
                    b, c = step
                    n = DC * (b - 1) + c
                    pool.wait_ge(v_klo, DC)
                    pool.wait_ge(a_khi, DC + n + 1)
                    pool.tensor_tensor(klo[b % 2][:, c, :], kblock[:, :, :].rearrange("p h k -> p (h k)"),
                                       khi[b % 2][:, c, :].bitcast(F32), ALU.subtract).then_inc(p_klo, 1)
                step = key_step(s)
                if step and step[0]:
                    b, c = step
                    pool.wait_ge(p_klo, DC * (b - 1) + c)
                    pool.wait_ge(v_klo, DC)
                    pool.tensor_tensor(kblock[:, :, :], *key_block(b, c), ALU.mult).then_inc(p_kblock, 1)
                g = xnT_group(s)
                if g is not None:
                    pool.wait_ge(a_xnT, g + 1)
                    pool.tensor_tensor(xnTlo[:, :, :], xnT[:, :, :], xnThi[:, :, :].bitcast(F32),
                                       ALU.subtract).then_inc(p_xnT, 1)
                g = q_group(s)
                if g is not None:
                    pool.wait_ge(a_q, g + 1)
                    pool.tensor_tensor(qTlo[g % 2][:, :, :], qT[:, :, :], qThi[g % 2][:, :, :].bitcast(F32),
                                       ALU.subtract).then_inc(p_q, 1)
                k = weight_piece(s)
                if k is not None:
                    pool.wait_ge(a_whi, k + 1)
                    pool.tensor_tensor(part_of(w1lo, k), raw[k % 2][:, :], part_of(w1hi, k).bitcast(F32),
                                       ALU.subtract).then_inc(p_wlo, 1)
            pool.wait_ge(v_logit, NT)
            for i in range(2):
                pool.wait_ge(d_xn2[i], 16 * (NT // 2))
            for i in range(XBUF):
                pool.wait_ge(d_x1[i], 16 * x1_stores[i])
            for k in range(E):
                pool.wait_ge(a_w2hi, k + 1)
                pool.tensor_tensor(part_of(w2lo, k), raw2[k % 2][:, :], part_of(w2hi, k).bitcast(F32),
                                   ALU.subtract).then_inc(p_w2lo, 1)
            pool.wait_ge(v_lists, 1)

            def gather(j):
                if j >= XG:
                    pool.wait_ge(t_xgT, j - XG + 1)
                pool.indirect_dma_start(xg[j % XG][:, :], None, xn2_dram[:, :],
                                        bass.IndirectOffsetOnAxis(ap=gather_at[:, j:j + 1], axis=0)).then_inc(d_xg[j % XG], 16)

            for j in range(XG - 1):
                gather(j)
            for j in range(NJ):
                if j + XG - 1 < NJ:
                    gather(j + XG - 1)
                pool.wait_ge(a_y, j + 1)
                pool.indirect_dma_start(y_dram[:, :], bass.IndirectOffsetOnAxis(ap=scatter_at[:, j:j + 1], axis=0),
                                        y_sb[j % 2][:, :], None).then_inc(d_ys[j % 2], 16)

        @block.scalar
        def _(act):
            act.dma_start(ctx_sb[:, :, :], ctx_in.rearrange("b k d -> k b d")).then_inc(d_ctx, 16)
            act.dma_start(wv_sb[:, :, :], wv.rearrange("(c p) n -> p c n", p=P)).then_inc(d_wv, 16)
            act.dma_start(gates[:, 0:1], g_xattn.partition_broadcast(P)).then_inc(d_gate, 16)
            act.dma_start(gates[:, 1:2], g_ffn.partition_broadcast(P)).then_inc(d_gate, 16)
            act.wait_ge(t_ctx, 1)
            act.activation(*ctx_copies(0), ACT.Copy).then_inc(a_ctxT, 1)
            act.wait_ge(d_wq, 16)
            act.activation(wqhi[:, :, :], wq_sb[:, :, :], ACT.Copy).then_inc(a_wq, 1)
            act.wait_ge(d_bk, 16 * DC)
            for c in range(DC):
                act.wait_ge(t_k, c + 1)
                act.activation(kT[:, c, :], bank[2 + c][:, 0:B * KEYS], ACT.Identity,
                               bias=bk_sb[:, c:c + 1]).then_inc(a_kT, 1)
            act.wait_ge(d_wo, 32)
            act.activation(wohi[:, :, :], wo_sb[:, :, :], ACT.Copy).then_inc(a_wo, 1)
            act.wait_ge(d_gate, 32)
            act.activation(tg[:, :], gates[:, :], ACT.Tanh).then_inc(a_tanh, 1)
            act.wait_ge(d_bq, 16 * DC)

            for s in SLOTS:
                u = unit(s - 1)
                if u is not None:
                    if u >= 2:
                        act.wait_ge(t_pv, u - 1)
                    act.wait_ge(t_probT, 2 * u + 1)
                    act.activation(probT[u % 2][:, 0:3, :].rearrange("p c n -> p (c n)"), t_bank[0][:, 0:3 * P],
                                   ACT.Copy).then_inc(a_probT, 1)
                    act.wait_ge(t_probT, 2 * u + 2)
                    act.activation(probT[u % 2][:, 3:KC, :].rearrange("p c n -> p (c n)"), t_bank[1][:, 0:(KC - 3) * P],
                                   ACT.Copy).then_inc(a_probT, 1)
                t = norm2_apply(s)
                if t is not None:
                    act.wait_ge(p_nr2, t + 1)
                    if t >= 2:
                        act.wait_ge(d_xn2[t % 2], 16 * (t // 2))
                        act.wait_ge(t_xn2T, t - 1)
                    act.activation(xn2[t % 2][:, :], xs[t // GT % XBUF][:, t % GT, :], ACT.Identity,
                                   bias=nr2[:, 0:1], scale=rs2[:, 0:1]).then_inc(a_xn2, 1)
                t = xn2T_tile(s)
                if t is not None:
                    act.wait_ge(t_xn2T, t + 1)
                    act.wait_ge(t_logit, t)
                    act.activation(xn2T[:, :, :], shared_place["xn2T", t][:, 0:D].rearrange("p (c n) -> p c n", n=P),
                                   ACT.Copy).then_inc(a_xn2T, 1)
                u = unit(s + 1)
                if u is not None:
                    act.wait_ge(v_sub, u + 1)
                    act.activation(prob[u % 2][:, 0:UC], prob[u % 2][:, 0:UC], ACT.Exp,
                                   scale=DH ** -0.5).then_inc(a_exp, 1)
                t = attnT_tile(s)
                if t is not None:
                    act.wait_ge(t_attnT, t + 1)
                    act.wait_ge(t_wo, t)
                    act.activation(attnThi[:, :, :], shared_place["attnT", t][:, 0:D].rearrange("p (c n) -> p c n", n=P),
                                   ACT.Copy).then_inc(a_attnT, 1)
                g = xnT_group(s)
                if g is not None:
                    act.wait_ge(t_xnT, g + 1)
                    act.wait_ge(p_xnT, g)
                    act.activation(xnT[:, :, :].rearrange("p c n -> p (c n)"), shared_place["xnT", g],
                                   ACT.Copy).then_inc(a_xnTf, 1)
                    act.wait_ge(a_xnTf, g + 1)
                    act.wait_ge(t_q, g)
                    act.activation(xnThi[:, :, :], xnT[:, :, :], ACT.Copy).then_inc(a_xnT, 1)
                g = q_group(s)
                if g is not None:
                    act.wait_ge(t_q, g + 1)
                    act.wait_ge(p_q, g)
                    for c in range(DC):
                        ins = act.activation(qT[:, c, :], shared_place["q", g][:, c * GT * P:(c + 1) * GT * P],
                                             ACT.Identity, bias=bq_sb[:, c:c + 1])
                    ins.then_inc(a_qf, 1)
                    act.wait_ge(a_qf, g + 1)
                    if g >= 2:
                        act.wait_ge(t_score, 2 * GT * (g - 1))
                    act.activation(qThi[g % 2][:, :, :], qT[:, :, :], ACT.Copy).then_inc(a_q, 1)
                g = norm1_apply(s)
                if g is not None:
                    act.wait_ge(p_nr1, g + 1)
                    act.wait_ge(d_x[g % XBUF], 16 * (g // XBUF + 1))
                    act.wait_ge(t_xnT, g)
                    for i in range(GT):
                        ins = act.activation(xn[:, i, :], xs[g % XBUF][:, i, :], ACT.Identity,
                                             bias=nr1[:, i:i + 1], scale=rs1[:, i:i + 1])
                    ins.then_inc(a_xn, 1)
                step = key_split(s)
                if step:
                    b, c = step
                    n = DC * b + c
                    if b:
                        act.wait_ge(p_kblock, n - DC + 1)
                    else:
                        act.wait_ge(v_kblock, n + 1)
                    act.activation(khi[b % 2][:, c, :], kblock[:, :, :].rearrange("p h k -> p (h k)"),
                                   ACT.Copy).then_inc(a_khi, 1)
                k = weight_piece(s)
                if k is not None:
                    act.wait_ge(d_raw[k % 2], 16 * (k // 2 + 1))
                    act.activation(part_of(w1hi, k), raw[k % 2][:, :], ACT.Copy).then_inc(a_whi, 1)
            act.wait_ge(v_lgm, 1)
            act.activation(prob8[:, :, :], lgm[:, :, :], ACT.Exp).then_inc(a_prob8, 1)
            for k in range(E):
                act.wait_ge(d_raw2[k % 2], 16 * (k // 2 + 1))
                act.activation(part_of(w2hi, k), raw2[k % 2][:, :], ACT.Copy).then_inc(a_w2hi, 1)
            def store_y(j):
                act.wait_ge(t_y, j + 1)
                if j >= 2:
                    act.wait_ge(d_ys[j % 2], 16 * (j // 2))
                act.activation(y_sb[j % 2][:, :], bank[6 + j % 2][:, 0:D], ACT.Copy).then_inc(a_y, 1)

            for j in range(-3, NJ + 1):
                if 0 <= j - 2:
                    store_y(j - 2)
                if 0 <= j < NJ:
                    act.wait_ge(t_hT, j + 1)
                    if j >= 2:
                        act.wait_ge(t_y, j - 1)
                    act.activation(hThi[j % 2][:, :, :].rearrange("p c n -> p (c n)"), bank[2 + j % 2][:, :],
                                   ACT.Copy).then_inc(a_hT, 1)
                if j + 3 < NJ:
                    i = j + 3
                    act.wait_ge(t_xgT, i + 1)
                    if i >= 2:
                        act.wait_ge(t_h, i - 1)
                    act.activation(xgThi[i % 2][:, :, :].rearrange("p c n -> p (c n)"), bank[4 + i % 2][:, 0:D],
                                   ACT.Copy).then_inc(a_xgT, 1)
                if 0 <= j + 2 < NJ:
                    i = j + 2
                    act.wait_ge(t_h, i + 1)
                    act.wait_ge(v_hsq, i)
                    act.activation(hrelu[:, :], bank[i % 2][:, :], ACT.Relu).then_inc(a_relu, 1)
            store_y(NJ - 1)

        @block.tensor
        def _(pe):
            def three_pass(dst, hi_l, lo_l, hi_r, lo_r, n):
                passes = [(l, r) for l, r in ((hi_l, hi_r), (hi_l, lo_r), (lo_l, hi_r))]
                for k in range(n):
                    for i, (l, r) in enumerate(passes):
                        mm = pe.matmul(dst, l(k), r(k), start=(k == 0 and i == 0), stop=(k == n - 1 and i == 2))
                return mm

            pe.wait_ge(d_const, 16)
            pe.wait_ge(d_ctx, 16)
            for c in range(DC):
                for b in range(B):
                    mm = pe.transpose(bank[c][:, b * KEYS:(b + 1) * KEYS], ctx_sb[:, b, c * P:(c + 1) * P],
                                      ident[0:KEYS, 0:KEYS])
                mm.then_inc(t_ctx, 1)
            pe.wait_ge(d_wk, 16)
            pe.wait_ge(a_ctxT, 1)
            pe.wait_ge(v_ctxT, 1)
            for c in range(DC):
                for d in range(DC):
                    mm = pe.matmul(bank[2 + c][:, 0:B * KEYS], wk_sb[:, d, c * P:(c + 1) * P],
                                   ctxT[:, d, :, 0:KEYS], start=(d == 0), stop=(d == DC - 1))
                mm.then_inc(t_k, 1)
            pe.wait_ge(v_bvw, 1)
            pe.wait_ge(d_wo, 32)
            for d in range(DC):
                mm = pe.matmul(bank[6][:, 0:D], bv_wide[:, d, :], wo_sb[:, d, :], start=(d == 0), stop=(d == DC - 1))
            mm.then_inc(t_bo, 1)
            pe.wait_ge(v_bo, 1)
            pe.wait_ge(d_wv, 16)

            shared_n = [0]

            def take_shared():
                if shared_n[0] >= 2:
                    what, n = shared_order[shared_n[0] - 2]
                    pe.wait_ge(drained_by[what], n + 1)
                shared_n[0] += 1

            for s in SLOTS:
                u = unit(s + 2)
                if u is not None:
                    t, c = divmod(u, 2)
                    g = t // GT
                    pe.wait_ge(p_q, g + 1)
                    if g < GPB:
                        pe.wait_ge(v_klo, c + 1)
                    else:
                        pe.wait_ge(p_klo, DC * (g // GPB - 1) + c + 1)
                    if u >= 2:
                        pe.wait_ge(v_sub, u - 1)
                    qs = slice(t % GT * P, t % GT * P + P)
                    b = g // GPB
                    for j in range(2):
                        js = slice(j * QC, (j + 1) * QC)
                        mm = three_pass(pair[u % 2][:, j, 0:QC],
                                        lambda k: qThi[g % 2][:, c, qs], lambda k: qTlo[g % 2][:, c, qs],
                                        lambda k: khi[b % 2][:, c, js], lambda k: klo[b % 2][:, c, js], 1)
                    mm.then_inc(t_score, 1)
                t = xn2T_tile(s)
                if t is not None:
                    take_shared()
                    pe.wait_ge(a_xn2, t + 1)
                    for c in range(DC):
                        mm = pe.transpose(shared_place["xn2T", t][:, c * P:(c + 1) * P],
                                          xn2[t % 2][:, c * P:(c + 1) * P], ident)
                    mm.then_inc(t_xn2T, 1)
                t = logit_tile(s)
                if t is not None:
                    take_shared()
                    pe.wait_ge(a_xn2T, t + 1)
                    for c in range(DC):
                        mm = pe.matmul(shared_place["logit", t][:, 0:E], xn2T[:, c, :], wg_sb[:, c, :],
                                       start=(c == 0), stop=(c == DC - 1))
                    mm.then_inc(t_logit, 1)
                u = unit(s - 1)
                if u is not None:
                    t, c = divmod(u, 2)
                    b = t // (NT // B)
                    pe.wait_ge(a_probT, 2 * u + 2)
                    pe.wait_ge(v_vals, (b + 1) * KC)
                    pe.wait_ge(v_ones, 1)
                    for i in range(KC):
                        mm = pe.matmul(v_bank[:, 0:UH * VW], probT[u % 2][:, i, :], vals[:, b, c, i, :],
                                       start=(i == 0), stop=(i == KC - 1))
                    mm.then_inc(t_pv, 1)
                t = attnT_tile(s)
                if t is not None:
                    take_shared()
                    pe.wait_ge(v_attn, 2 * t + 2)
                    for c in range(DC):
                        mm = pe.transpose(shared_place["attnT", t][:, c * P:(c + 1) * P], attn[:, c * P:(c + 1) * P], ident)
                    mm.then_inc(t_attnT, 1)
                t = wo_tile(s)
                if t is not None:
                    take_shared()
                    pe.wait_ge(v_attnT, t + 1)
                    pe.wait_ge(p_wqo, 2)
                    mm = three_pass(shared_place["wo", t][:, 0:D], lambda k: attnThi[:, k, :], lambda k: attnTlo[:, k, :],
                                    lambda k: wohi[:, k, :], lambda k: wolo[:, k, :], DC)
                    mm.then_inc(t_wo, 1)
                g = xnT_group(s)
                if g is not None:
                    take_shared()
                    pe.wait_ge(a_xn, g + 1)
                    for c in range(DC):
                        for i in range(GT):
                            mm = pe.transpose(shared_place["xnT", g][:, (c * GT + i) * P:(c * GT + i + 1) * P],
                                              xn[:, i, c * P:(c + 1) * P], ident)
                    mm.then_inc(t_xnT, 1)
                g = q_group(s)
                if g is not None:
                    take_shared()
                    pe.wait_ge(p_xnT, g + 1)
                    pe.wait_ge(p_wqo, 1)
                    for c in range(DC):
                        cs = slice(c * P, (c + 1) * P)
                        mm = three_pass(shared_place["q", g][:, c * GT * P:(c + 1) * GT * P],
                                        lambda k: wqhi[:, k, cs], lambda k: wqlo[:, k, cs],
                                        lambda k: xnThi[:, k, :], lambda k: xnTlo[:, k, :], DC)
                    mm.then_inc(t_q, 1)
                n = value_step(s)
                if n is not None:
                    b, i = divmod(n, KC)
                    take_shared()
                    dst = shared_place["value", n][:, 0:2 * WIN * DH].rearrange("p (c n) -> p c n", c=2)
                    at0 = P * i % KEYS
                    for d in range(DC):
                        cols = wv_sb[:, d, :].rearrange("p (c h e) -> p c (h e)", c=2, e=DH)
                        mm = pe.matmul(dst, ctxT[:, d, b, at0:at0 + P], cols[:, :, HEAD0[i] * DH:(HEAD0[i] + WIN) * DH],
                                       start=(d == 0), stop=(d == DC - 1))
                    mm.then_inc(t_v, 1)
                u = unit(s)
                if u is not None:
                    pe.wait_ge(a_exp, u + 1)
                    if u:
                        pe.wait_ge(a_probT, 2 * u)
                    for i in range(KC):
                        tb = t_bank[i // 3]
                        if i == 3 and u:
                            pe.wait_ge(v_attn, u)
                        mm = pe.transpose(tb[:, (i % 3) * P:(i % 3 + 1) * P], prob[u % 2][:, i * P:(i + 1) * P], ident)
                        if i in (2, KC - 1):
                            mm.then_inc(t_probT, 1)

            pe.wait_ge(v_pick, 1)
            pickf = slot_te[:, :, :].rearrange("p t e -> p (t e)")
            pe.matmul(bank[0][:, 0:NT * E], C("before"), pickf, start=True, stop=True)
            pe.matmul(bank[1][:, 0:NT * E], ones[:, :], pickf, start=True, stop=True).then_inc(t_rank, 1)
            for q in range(NC // PART):
                pe.wait_ge(v_tile, q + 1)
                for i in range(PART):
                    n = q * PART + i
                    mm = pe.matmul(bank[2 + n // NT][:, 0:2 * NJ], onehot_row[q % 2][:, i, :], onehot_tile[q % 2][:, i, :],
                                   start=(n % NT == 0), stop=(n % NT == NT - 1))
                mm.then_inc(t_list, 1)

            pe.wait_ge(v_lists, 1)
            pe.wait_ge(p_wlo, E)
            pe.wait_ge(p_w2lo, E)
            expert = [None] * NJ
            for j in range(-3, NJ + 1):
                if 0 <= j < NJ:
                    pe.wait_ge(v_hsq, j + 1)
                    if j >= 2:
                        pe.wait_ge(v_hT, j - 1)
                    for c in range(HC):
                        mm = pe.transpose(bank[2 + j % 2][:, c * P:(c + 1) * P], hsq[j % 2][:, c * P:(c + 1) * P], ident)
                    mm.then_inc(t_hT, 1)
                if j + 3 < NJ:
                    i = j + 3
                    pe.wait_ge(d_xg[i % XG], 16 * (i // XG + 1))
                    if i >= 2:
                        pe.wait_ge(v_xgT, i - 1)
                    for c in range(DC):
                        mm = pe.transpose(bank[4 + i % 2][:, c * P:(c + 1) * P], xg[i % XG][:, c * P:(c + 1) * P], ident)
                    mm.then_inc(t_xgT, 1)
                if 0 <= j + 2 < NJ:
                    i = j + 2
                    expert[i] = pe.value_load(expert_at[0:1, i:i + 1], min_val=0, max_val=(E - 1) * EW)
                    pe.wait_ge(v_xgT, i + 1)
                    if i >= 2:
                        pe.wait_ge(v_hsq, i - 1)
                    w = lambda part, k: part[:, bass.ds(expert[i] + k * H, H)]
                    mm = three_pass(bank[i % 2][:, :], lambda k: xgThi[i % 2][:, k, :], lambda k: xgTlo[i % 2][:, k, :],
                                    lambda k: w(w1hi, k), lambda k: w(w1lo, k), DC)
                    mm.then_inc(t_h, 1)
                if 0 <= j - 1:
                    i = j - 1
                    pe.wait_ge(v_hT, i + 1)
                    if i >= 2:
                        pe.wait_ge(a_y, i - 1)
                    w = lambda part, k: part[:, bass.ds(expert[i] + k * D, D)]
                    mm = three_pass(bank[6 + i % 2][:, 0:D], lambda k: hThi[i % 2][:, k, :], lambda k: hTlo[i % 2][:, k, :],
                                    lambda k: w(w2hi, k), lambda k: w(w2lo, k), HC)
                    mm.then_inc(t_y, 1)

        @block.vector
        def _(dve):
            own = [0]

            def link(ins):
                own[0] += 1
                ins.then_inc(v_own, 1)
                dve.wait_ge(v_own, own[0])

            for i in range(2):
                dve.memset(prob[i][:, UC:UPAD], 0.0).then_inc(v_init, 1)
            dve.wait_ge(d_const, 16)
            dve.wait_ge(p_init, 3)
            for i in range(KC):
                heads = vals[:, :, :, i, :].rearrange("p b c (h e) -> p (b c) h e", e=VW)
                ins = dve.tensor_copy(heads[:, :, HEAD0[i]:HEAD0[i] + WIN, DH],
                                      C("vmask")[:, i * WIN:(i + 1) * WIN].unsqueeze(1).broadcast_to([P, 2 * B, WIN]))
            ins.then_inc(v_ones, 1)
            dve.wait_ge(t_ctx, 2)
            dve.tensor_copy(*ctx_copies(1)).then_inc(v_ctxT, 1)
            dve.wait_ge(d_bv, 16 * DC)
            dve.tensor_copy(bv_wide[:, :, :], bv_sb[:, :].unsqueeze(2).broadcast_to([P, DC, P])).then_inc(v_bvw, 1)
            dve.wait_ge(d_bo, 16)
            dve.wait_ge(t_bo, 1)
            dve.wait_ge(a_tanh, 1)
            link(dve.tensor_tensor(bo_sb[:, :], bank[6][:, 0:D], bo_sb[:, :], ALU.add))
            dve.tensor_scalar(bo_sb[:, :], bo_sb[:, :], tg[:, 0:1], None, ALU.mult).then_inc(v_bo, 1)

            for s in SLOTS:
                u1 = unit(s + 1)
                if u1 is not None:
                    dve.wait_ge(t_score, u1 + 1)
                    dve.wait_ge(v_sub, u1)
                    scores = pair[u1 % 2][:, :, 0:QC].rearrange("p j (h k) -> p j h k", k=KEYS)
                    dve.tensor_reduce(rowmax[:, :].rearrange("p (j h) -> p j h", j=2), scores, AX.X,
                                      ALU.max).then_inc(v_max, 1)
                t2 = norm2_stats(s)
                if t2 is not None:
                    dve.wait_ge(v_x1, t2 + 1)
                    dve.bn_stats(st2[:, :], xs[t2 // GT % XBUF][:, t2 % GT, :]).then_inc(v_bn2, 1)
                if u1 is not None:
                    dve.wait_ge(v_max, u1 + 1)
                    if u1 >= 2:
                        dve.wait_ge(t_probT, 2 * (u1 - 1))
                    dve.tensor_tensor(prob[u1 % 2][:, 0:UC].rearrange("p (j h k) -> p j h k", j=2, k=KEYS), scores,
                                      rowmax[:, :].rearrange("p (j h) -> p j h", j=2).unsqueeze(3)
                                      .broadcast_to([P, 2, QH, KEYS]), ALU.subtract).then_inc(v_sub, 1)
                if t2 is not None:
                    dve.wait_ge(v_bn2, t2 + 1)
                    dve.wait_ge(p_nr2, t2)
                    dve.bn_aggr(mv2[:, :], st2[:, :]).then_inc(v_var2, 1)
                t = logit_tile(s)
                if t is not None:
                    dve.wait_ge(t_logit, t + 1)
                    dve.tensor_copy(logits[:, t, :], shared_place["logit", t][:, 0:E]).then_inc(v_logit, 1)
                u = unit(s - 1)
                if u is not None:
                    t, c = divmod(u, 2)
                    dve.wait_ge(t_pv, u + 1)
                    dve.wait_ge(v_attn, u)
                    pv = v_bank[:, 0:UH * VW].rearrange("p (h e) -> p h e", e=VW)
                    dve.reciprocal(recip[:, :], pv[:, :, DH]).then_inc(v_recip, 1)
                g = norm1_stats(s)
                if g is not None:
                    dve.wait_ge(d_x[g % XBUF], 16 * (g // XBUF + 1))
                    dve.wait_ge(p_nr1, g)
                    dve.wait_ge(v_var1, g)
                    for i in range(GT):
                        ins = dve.bn_stats(st1[:, i, :], xs[g % XBUF][:, i, :])
                    ins.then_inc(v_bn1, 1)
                if u is not None:
                    dve.wait_ge(v_recip, u + 1)
                    if c == 0 and t:
                        dve.wait_ge(t_attnT, t)
                    dve.tensor_tensor(attn[:, c * P:(c + 1) * P].rearrange("p (h e) -> p h e", e=DH),
                                      pv[:, :, 0:DH], recip[:, :].unsqueeze(2).broadcast_to([P, UH, DH]),
                                      ALU.mult).then_inc(v_attn, 1)
                t = attnT_tile(s)
                if t is not None:
                    dve.wait_ge(a_attnT, t + 1)
                    dve.tensor_tensor(attnTlo[:, :, :], shared_place["attnT", t][:, 0:D].rearrange("p (c n) -> p c n", n=P),
                                      attnThi[:, :, :].bitcast(F32), ALU.subtract).then_inc(v_attnT, 1)
                n = value_step(s)
                if n is not None:
                    b, i = divmod(n, KC)
                    dve.wait_ge(t_v, n + 1)
                    mask = C("vmask")[:, i * WIN:(i + 1) * WIN]
                    heads = vals[:, b, :, i, :].rearrange("p c (h e) -> p c h e", e=VW)
                    dve.tensor_tensor(heads[:, :, HEAD0[i]:HEAD0[i] + WIN, 0:DH],
                                      shared_place["value", n][:, 0:2 * WIN * DH].rearrange("p (c w e) -> p c w e", c=2, e=DH),
                                      mask.unsqueeze(1).unsqueeze(3).broadcast_to([P, 2, WIN, DH]), ALU.mult).then_inc(v_vals, 1)
                if g is not None:
                    dve.wait_ge(v_bn1, g + 1)
                    for i in range(GT):
                        ins = dve.bn_aggr(mv1[:, i, :], st1[:, i, :])
                    ins.then_inc(v_var1, 1)
                t = wo_tile(s)
                if t is not None:
                    x1 = xs[t // GT % XBUF][:, t % GT, :]
                    dve.wait_ge(t_wo, t + 1)
                    dve.wait_ge(p_xb, t // GT + 1)
                    dve.scalar_tensor_tensor(out=x1, in0=shared_place["wo", t][:, 0:D], scalar=tg[:, 0:1], in1=x1,
                                             op0=ALU.mult, op1=ALU.add).then_inc(v_x1, 1)
                step = key_step(s)
                if step and step[0] == 0:
                    c = step[1]
                    dve.wait_ge(a_kT, c + 1)
                    dve.wait_ge(v_klo, c)
                    dve.tensor_tensor(kblock[:, :, :], *key_block(0, c), ALU.mult).then_inc(v_kblock, 1)
                    dve.wait_ge(a_khi, c + 1)
                    dve.tensor_tensor(klo[0][:, c, :], kblock[:, :, :].rearrange("p h k -> p (h k)"),
                                      khi[0][:, c, :].bitcast(F32), ALU.subtract).then_inc(v_klo, 1)

            TE = [P, NT, E]
            over_e = lambda a: a.unsqueeze(2).broadcast_to(TE)
            over_t = lambda a: a.unsqueeze(1).broadcast_to(TE)
            tt = lambda *a: link(dve.tensor_tensor(*a))
            ts = lambda *a: link(dve.tensor_scalar(*a))
            dve.wait_ge(v_logit, NT)
            dve.wait_ge(p_wlo, E)
            for i in range(2):
                dve.wait_ge(d_xn2[i], 16 * (NT // 2))
            for i in range(XBUF):
                dve.wait_ge(d_x1[i], 16 * x1_stores[i])
            best, second, key, tmp = top[:, 0, :], top[:, 1, :], small[:, 0, :], small[:, 1, :]

            def choose(values, best_of, chosen):
                link(dve.tensor_reduce(best_of, values, AX.X, ALU.max))
                tt(chosen, values, over_e(best_of), ALU.is_equal)
                tt(chosen, chosen, over_t(C("lowest")), ALU.mult)
                link(dve.tensor_reduce(key, chosen, AX.X, ALU.max))
                tt(chosen, chosen, over_e(key), ALU.is_equal)

            choose(logits[:, :, :], best, pick[0][:, :, :])
            dve.tensor_tensor(lgm[:, :, :], logits[:, :, :], over_e(best), ALU.subtract).then_inc(v_lgm, 1)
            dve.wait_ge(v_lgm, 1)
            link(dve.tensor_reduce(tmp, lgm[:, :, :], AX.X, ALU.min))
            ts(tmp, tmp, 2.0, -1.0, ALU.mult, ALU.add)
            tt(count[0][:, :, :], pick[0][:, :, :], over_e(tmp), ALU.mult)
            tt(count[0][:, :, :], count[0][:, :, :], lgm[:, :, :], ALU.add)
            choose(count[0][:, :, :], second, pick[1][:, :, :])
            dve.tensor_tensor(slot_te[:, :, :], pick[0][:, :, :], pick[1][:, :, :], ALU.add).then_inc(v_pick, 1)
            dve.wait_ge(a_prob8, 1)
            link(dve.tensor_reduce(small[:, 2, :], prob8[:, :, :], AX.X, ALU.add))
            link(dve.reciprocal(small[:, 2, :], small[:, 2, :]))
            tt(prob8[:, :, :], prob8[:, :, :], over_e(small[:, 2, :]), ALU.mult)
            for k in range(CHOICES):
                tt(count[1][:, :, :], prob8[:, :, :], pick[k][:, :, :], ALU.mult)
                link(dve.tensor_reduce(tile_w[:, k, :], count[1][:, :, :], AX.X, ALU.add))
            tt(small[:, 3, :], tile_w[:, 0, :], tile_w[:, 1, :], ALU.add)
            ts(small[:, 3, :], small[:, 3, :], 1e-8, None, ALU.add)
            link(dve.reciprocal(small[:, 3, :], small[:, 3, :]))
            tt(tile_w[:, :, :], tile_w[:, :, :], small[:, 3, :].unsqueeze(1).broadcast_to([P, CHOICES, NT]), ALU.mult)
            ts(tile_w[:, :, :], tile_w[:, :, :], tg[:, 1:2], None, ALU.mult)
            dve.wait_ge(t_rank, 1)
            of_tile = totals[:, :, :]
            link(dve.tensor_copy(of_tile.rearrange("p t e -> p (t e)"), bank[1][:, 0:NT * E]))
            link(dve.tensor_copy(count[0][:, :, :], of_tile))
            src, dst = count
            step = 1
            while step < NT:
                link(dve.tensor_copy(dst[:, 0:step, :], src[:, 0:step, :]))
                tt(dst[:, step:, :], src[:, step:, :], src[:, :NT - step, :], ALU.add)
                src, dst = dst, src
                step *= 2
            tt(dst[:, :, :], over_t(src[:, NT - 1, :]), over_e(C("full")), ALU.is_gt)
            link(dve.tensor_reduce(need[:, :], dst[:, :, :].rearrange("p t e -> p e t"), AX.X, ALU.add))
            link(dve.tensor_copy(first[0][:, :], need[:, :]))
            f, f2 = first
            step = 1
            while step < E:
                link(dve.tensor_copy(f2[:, 0:step], f[:, 0:step]))
                tt(f2[:, step:], f[:, step:], f[:, :E - step], ALU.add)
                f, f2 = f2, f
                step *= 2
            tt(ended[:, :, :], f[0:1, 0:E - 1].unsqueeze(1).broadcast_to([1, NJ, E - 1]),
               C("iota")[0:1, 0:NJ].unsqueeze(2).broadcast_to([1, NJ, E - 1]), ALU.is_le)
            link(dve.tensor_reduce(listf[0:1, 0, :], ended[:, :, :], AX.X, ALU.add))
            ts(expert_at[:, :], listf[0:1, 0, :], float(EW), None, ALU.mult)
            tt(f2[:, :], f[:, :], need[:, :], ALU.subtract)
            ts(base[:, :], f2[:, :], float(P), None, ALU.mult)
            tt(src[:, :, :], src[:, :, :], of_tile, ALU.subtract)
            tt(src[:, :, :], src[:, :, :], over_t(base[:, :]), ALU.add)
            tt(src[:, :, :], src[:, :, :], bank[0][:, 0:NT * E].rearrange("p (t e) -> p t e", e=E), ALU.add)
            for k in range(CHOICES):
                tt(dst[:, :, :], src[:, :, :], pick[k][:, :, :], ALU.mult)
                link(dve.tensor_reduce(slot[:, k, :], dst[:, :, :], AX.X, ALU.add))
            link(dve.tensor_copy(slot_i[:, :], slot[:, :, :].rearrange("p k t -> p (k t)")))
            ts(srow_i[:, :], slot_i[:, :], P - 1, None, ALU.bitwise_and)
            ts(stile_i[:, :], slot_i[:, :], P.bit_length() - 1, None, ALU.logical_shift_right)
            link(dve.tensor_copy(srow[:, :], srow_i[:, :]))
            link(dve.tensor_copy(stile[:, :], stile_i[:, :]))
            for q in range(NC // PART):
                ns = slice(q * PART, (q + 1) * PART)
                if q >= 2:
                    dve.wait_ge(t_list, q - 1)
                dve.tensor_tensor(onehot_row[q % 2][:, :, :], srow[:, ns].unsqueeze(2).broadcast_to([P, PART, P]),
                                  C("iota").unsqueeze(1).broadcast_to([P, PART, P]), ALU.is_equal)
                hit = onehot_tile[q % 2][:, :, NJ:2 * NJ]
                tt(hit, stile[:, ns].unsqueeze(2).broadcast_to([P, PART, NJ]),
                   C("iota")[:, 0:NJ].unsqueeze(1).broadcast_to([P, PART, NJ]), ALU.is_equal)
                t0 = q * PART % NT
                dve.tensor_tensor(onehot_tile[q % 2][:, :, 0:NJ], hit.bitcast(F32),
                                  C("token")[:, t0:t0 + PART].unsqueeze(2).broadcast_to([P, PART, NJ]),
                                  ALU.mult).then_inc(v_tile, 1)
            dve.wait_ge(t_list, NC // PART)
            link(dve.tensor_copy(listed[:, :], bank[2][:, 0:2 * NJ]))
            tok, filled, row = listf[:, 0, :], listf[:, 1, :], listf[:, 2, :]
            tt(tok, listed[:, 0:NJ], bank[3][:, 0:NJ], ALU.add)
            tt(filled, listed[:, NJ:2 * NJ], bank[3][:, NJ:2 * NJ], ALU.add)
            link(dve.scalar_tensor_tensor(out=row, in0=tok, scalar=2.0, in1=bank[3][:, NJ:2 * NJ], op0=ALU.mult, op1=ALU.add))
            ts(filled, filled, -1.0, 1.0, ALU.mult, ALU.add)
            tt(filled, filled, C("spare"), ALU.mult)
            tt(row, row, filled, ALU.add)
            link(dve.tensor_copy(gather_at[:, :], tok))
            dve.tensor_copy(scatter_at[:, :], row).then_inc(v_lists, 1)

            for j in range(-3, NJ):
                if 0 <= j:
                    dve.wait_ge(a_hT, j + 1)
                    dve.tensor_tensor(hTlo[j % 2][:, :, :].rearrange("p c n -> p (c n)"), bank[2 + j % 2][:, :],
                                      hThi[j % 2][:, :, :].rearrange("p c n -> p (c n)").bitcast(F32),
                                      ALU.subtract).then_inc(v_hT, 1)
                if j + 3 < NJ:
                    i = j + 3
                    dve.wait_ge(a_xgT, i + 1)
                    dve.tensor_tensor(xgTlo[i % 2][:, :, :].rearrange("p c n -> p (c n)"), bank[4 + i % 2][:, 0:D],
                                      xgThi[i % 2][:, :, :].rearrange("p c n -> p (c n)").bitcast(F32),
                                      ALU.subtract).then_inc(v_xgT, 1)
                if 0 <= j + 2 < NJ:
                    i = j + 2
                    dve.wait_ge(a_relu, i + 1)
                    if i >= 2:
                        dve.wait_ge(t_hT, i - 1)
                    dve.tensor_tensor(hsq[i % 2][:, :], bank[i % 2][:, :], hrelu[:, :], ALU.mult).then_inc(v_hsq, 1)

            dve.wait_ge(d_x1all, 16)
            for c in range(NT // CT):
                dve.wait_ge(d_yin[c], 16)
                for k in range(CHOICES):
                    for i in range(CT):
                        t = c * CT + i
                        ins = dve.scalar_tensor_tensor(out=x1_all[:, t, :], in0=y_in[c][:, i, k, :],
                                                       scalar=tile_w[:, k, t:t + 1], in1=x1_all[:, t, :],
                                                       op0=ALU.mult, op1=ALU.add)
                    if k < CHOICES - 1:
                        link(ins)
                ins.then_inc(v_out, 1)


_INS = ["x", "ctx_1024", "g_xattn", "g_ffn", "L0_xattn_Wq", "L0_xattn_Wk", "L0_xattn_Wv", "L0_xattn_Wo",
        "L0_xattn_bq", "L0_xattn_bk", "L0_xattn_bv", "L0_xattn_bo", "L0_ffn_Wg", "L0_ffn_W1", "L0_ffn_W2"]


def kernel(**inputs):
    import numpy as _np
    import concourse.bacc as _bacc
    from concourse import mybir as _mybir
    from concourse.bass_utils import run_bass_kernel_spmd as _run

    nc = _bacc.Bacc("TRN2", target_bir_lowering=False, num_devices=1)
    arrays, args = {}, []
    for name in _INS:
        a = _np.ascontiguousarray(inputs[name])
        arrays[f"in_{name}"] = a
        args.append(nc.dram_tensor(f"in_{name}", a.shape, _mybir.dt.from_np(a.dtype), kind="ExternalInput").ap())
    table = constants()[0]
    arrays["in_constants"] = table
    args.append(nc.dram_tensor("in_constants", table.shape, _mybir.dt.float32, kind="ExternalInput").ap())
    args.append(nc.dram_tensor("out", (B, S, D), _mybir.dt.float32, kind="ExternalOutput").ap())
    build(nc, *args)
    r = _run(nc, [arrays], core_ids=[0])
    return r.results[0]["out"]
```

```python
from contextlib import ExitStack

import numpy as np
import concourse.bass as bass
from concourse import mybir

F32 = mybir.dt.float32
F32R = mybir.dt.float32r
BF16 = mybir.dt.bfloat16
I32 = mybir.dt.int32
ALU = mybir.AluOpType
ACT = mybir.ActivationFunctionType
AX = mybir.AxisListType

P = 128
B, S, D = 4, 1024, 256
KEYS = 77
HEADS, DH = 16, 16
E, H = 8, 512
EPS = 1e-5
LOW = -3e38

N = B * S
NT = N // P
DC = D // P
HC = H // P
UNITS = 2 * NT
UH = HEADS // 2
UC = UH * KEYS
QH = UH // 2
QC = QH * KEYS
KC = -(-UC // P)
UPAD = KC * P
WIN = 3
VW = DH + 1
HEAD0 = [min(P * i // KEYS, UH - WIN) for i in range(KC)]
GT = 2
NG = NT // GT
GPB = NG // B
CHOICES = 2
NJ = (CHOICES * N + E * (P - 1)) // P
NJE = NJ + NJ % 2
NC = NT * CHOICES
XBUF = 5
XG = 9
PART = NT // 2
TP = PART // 2
W2BUF = 4
CT = 4
RL = 4
HW = 512


def constants():
    p = np.arange(P)[:, None]
    row = np.arange(P)[None, :]
    head = [(P * i + p) // KEYS for i in range(KC)]
    parts = {
        "ident": p == row,
        "before": p < row,
        "kmask": p // DH == np.arange(UH)[None, :],
        "vmask": np.concatenate([head[i] == HEAD0[i] + np.arange(WIN)[None, :] for i in range(KC)], 1),
        "lowest": E - np.arange(E)[None, :] + 0 * p,
        "iota": row + 0 * p,
        "token": P * np.arange(NT)[None, :] + p + 1,
        "spare": CHOICES * N + P * np.arange(NJ)[None, :] + p + CHOICES,
        "upto": np.concatenate([np.arange(E)[None, :] <= e for e in range(E)]
                               + [np.arange(E)[None, :] < e for e in range(E)], 1) + 0 * p,
    }
    at, cols = {}, 0
    for name, a in parts.items():
        at[name] = (cols, cols + a.shape[1])
        cols += a.shape[1]
    return np.concatenate([a.astype(np.float32) for a in parts.values()], 1), at


def build(nc, x, ctx_in, g_xattn, g_ffn, wq, wk, wv, wo, bq, bk, bv, bo, wg, w1, w2, consts, out):
    _, at = constants()
    x1_dram = nc.dram_tensor("x1_scratch", (N, D), F32).ap()
    xn2_dram = nc.dram_tensor("xn2_scratch", (N, D), F32).ap()
    y_dram = nc.dram_tensor("y_scratch", (CHOICES * N + NJ * P, D), F32).ap()

    rows = lambda a: a.rearrange("(t p) d -> p t d", p=P)
    x_rows = rows(x.rearrange("b s d -> (b s) d"))
    out_rows = rows(out.rearrange("b s d -> (b s) d"))
    x1_rows = rows(x1_dram)
    y_rows = y_dram[0:CHOICES * N, :].rearrange("(t p k) d -> p t k d", p=P, k=CHOICES)

    ctx = ExitStack()
    with ctx:
        def sem(name):
            return ctx.enter_context(nc.semaphore(name))

        def place(stack, name, shape, dt=F32):
            return stack.enter_context(nc.sbuf_tensor(name, shape, dt))

        cst = place(ctx, "cst", [P, at["iota"][0]])
        C = lambda name: cst[:, at[name][0]:at[name][1]]
        ident = C("ident")
        counters = place(ctx, "counters", [P, 2, P], BF16)
        logits = place(ctx, "logits", [P, NT, E])
        gates = place(ctx, "gates", [P, 2])
        tg = place(ctx, "tg", [P, 2])
        pick = place(ctx, "pick", [P, CHOICES, NT, E], BF16)
        best = place(ctx, "best", [P, CHOICES, NT])
        rank = place(ctx, "rank", [P, CHOICES, NT])
        chosen = place(ctx, "chosen", [P, GT, E])
        masked = place(ctx, "masked", [P, GT, E])
        key = place(ctx, "key", [P, GT])
        both = place(ctx, "both", [P, GT, E], BF16)
        place_te = place(ctx, "place_te", [P, GT, E])
        placed = place(ctx, "placed", [P, CHOICES, GT, E])
        count = place(ctx, "count", [P, E])
        w1hi = place(ctx, "w1hi", [P, E * DC * H], F32R)
        w1lo = place(ctx, "w1lo", [P, E * DC * H], F32R)
        EW = DC * H
        with ExitStack() as early:
            ctx_sb = place(early, "ctx_sb", [KEYS, B, D])
            ctxT = place(early, "ctxT", [P, DC, B, 3 * KEYS])
            wk_sb = place(early, "wk_sb", [P, DC, D])
            wv_sb = place(early, "wv_sb", [P, DC, D])
            wq_sb = place(early, "wq_sb", [P, DC, D])
            bv_sb = place(early, "bv_sb", [P, DC])
            bv_wide = place(early, "bv_wide", [P, DC, P])
            wo_sb = place(early, "wo_sb", [P, DC, D])
        w2hi = place(ctx, "w2hi", [P, E * HC * D], F32R)
        raw = [place(ctx, f"raw{i}", [P, EW]) for i in range(2)]
        tile_w = place(ctx, "tile_w", [P, CHOICES, NT])
        gather_at = place(ctx, "gather_at", [P, NJ], I32)
        scatter_at = place(ctx, "scatter_at", [P, NJ], I32)
        expert_at = place(ctx, "expert_at", [1, NJ], I32)

        with ExitStack() as a:
            kT = place(a, "kT", [P, DC, B * KEYS])
            kblock = place(a, "kblock", [P, UH, KEYS])
            khi = [place(a, f"khi{i}", [P, DC, UC], F32R) for i in range(2)]
            klo = [place(a, f"klo{i}", [P, DC, UC], F32R) for i in range(2)]
            vals = place(a, "vals", [P, B, 2, KC, UH * VW])
            wqhi = place(a, "wqhi", [P, DC, D], F32R)
            wqlo = place(a, "wqlo", [P, DC, D], F32R)
            wohi = place(a, "wohi", [P, DC, D], F32R)
            wolo = place(a, "wolo", [P, DC, D], F32R)
            wg_sb = place(a, "wg_sb", [P, DC, E])
            bo_sb = place(a, "bo_sb", [P, D])
            bq_sb = place(a, "bq_sb", [P, DC])
            bk_sb = place(a, "bk_sb", [P, DC])
            xs = [place(a, f"xs{i}", [P, GT, D]) for i in range(XBUF)]
            xn = place(a, "xn", [P, GT, D])
            xnT = place(a, "xnT", [P, DC, GT * P])
            qT = place(a, "qT", [P, DC, GT * P])
            xnThi = place(a, "xnThi", [P, DC, GT * P], F32R)
            xnTlo = place(a, "xnTlo", [P, DC, GT * P], F32R)
            qThi = [place(a, f"qThi{i}", [P, DC, GT * P], F32R) for i in range(2)]
            qTlo = [place(a, f"qTlo{i}", [P, DC, GT * P], F32R) for i in range(2)]
            prob = [place(a, f"prob{i}", [P, UPAD]) for i in range(2)]
            probT = [place(a, f"probT{i}", [P, KC, P]) for i in range(2)]
            attn = place(a, "attn", [P, D])
            attnThi = place(a, "attnThi", [P, DC, P], F32R)
            attnTlo = place(a, "attnTlo", [P, DC, P], F32R)
            xn2 = place(a, "xn2", [P, D])
            xn2T = place(a, "xn2T", [P, DC, P])
            rowmax = place(a, "rowmax", [P, UH])
            recip = place(a, "recip", [P, UH])
            st1 = place(a, "st1", [P, GT, 6])
            mv1 = place(a, "mv1", [P, GT, 2])
            ve1 = place(a, "ve1", [P, GT])
            rs1 = place(a, "rs1", [P, GT])
            nm1 = place(a, "nm1", [P, GT])
            nr1 = place(a, "nr1", [P, GT])
            st2 = place(a, "st2", [P, 6])
            mv2 = place(a, "mv2", [P, 2])
            ve2 = place(a, "ve2", [P, 1])
            rs2 = place(a, "rs2", [P, 1])
            nm2 = place(a, "nm2", [P, 1])
            nr2 = place(a, "nr2", [P, 1])
            exponent = place(a, "exponent", [P, GT])
        w2lo = place(ctx, "w2lo", [P, E * HC * D], F32R)
        with ExitStack() as r:
            cst2 = place(r, "cst2", [P, consts.shape[1] - at["iota"][0]])
            C2 = lambda name: cst2[:, at[name][0] - at["iota"][0]:at[name][1] - at["iota"][0]]
            ended = place(r, "ended", [1, NJ, E - 1])
            ended_n = place(r, "ended_n", [1, NJ])
            bounds = place(r, "bounds", [P, 2 * E])
            code0 = place(r, "code0", [P, NJ])
            code = place(r, "code", [P, NJ])
            second = place(r, "second", [P, NJ])
            yrow = place(r, "yrow", [P, NJ])
            empty = place(r, "empty", [P, NJ])
            need_i = [place(r, f"need_i{i}", [P, E], I32) for i in range(2)]
            need = place(r, "need", [P, E])
            sums = place(r, "sums", [P, 2 * E, E])
            picked = place(r, "picked", [P, CHOICES * NT, E])
            rank_i = place(r, "rank_i", [P, NC], I32)
            row_i = place(r, "row_i", [P, NC], I32)
            tile_i = place(r, "tile_i", [P, NC], I32)
            first_of = place(r, "first_of", [P, NC])
            tile_of = place(r, "tile_of", [P, NC])
            onehot_row = [place(r, f"onehot_row{i}", [P, PART, P], F32R) for i in range(2)]
            onehot_tile = [place(r, f"onehot_tile{i}", [P, PART, NJE], F32R) for i in range(2)]
            hit = [place(r, f"hit{i}", [P, PART, NJE]) for i in range(2)]
            raw2 = raw + [place(r, f"raw{i}", [P, EW]) for i in range(2, W2BUF)]
        with ExitStack() as m:
            x1_all = place(m, "x1_all", [P, NT, D])
            xg = [place(m, f"xg{i}", [P, D]) for i in range(XG)]
            xgThi = [place(m, f"xgThi{i}", [P, DC, P], F32R) for i in range(2)]
            xgTlo = [place(m, f"xgTlo{i}", [P, DC, P], F32R) for i in range(2)]
            hrelu = place(m, "hrelu", [P, H])
            hsq = [place(m, f"hsq{i}", [P, H]) for i in range(2)]
            hThi = [place(m, f"hThi{i}", [P, HC, P], F32R) for i in range(2)]
            hTlo = [place(m, f"hTlo{i}", [P, HC, P], F32R) for i in range(2)]
            weight8 = place(m, "weight8", [P, NT, E])
            weighed = place(m, "weighed", [P, CHOICES, NT, E])
            total = place(m, "total", [P, NT])
            y_sb = [place(m, f"y_sb{i}", [P, D]) for i in range(2)]
        YW = CT * CHOICES * D
        y_in = [w[:, i * YW:(i + 1) * YW].bitcast(F32).rearrange("p (t k d) -> p t k d", k=CHOICES, d=D)
                for w in (w1hi, w1lo) for i in range(E * EW // YW)]

        pair = [ctx.enter_context(nc.psum_tensor(f"pair{i}", [P, 2, HW], F32)) for i in range(4)]
        bank = [pair[i // 2][:, i % 2, :] for i in range(8)]
        t_bank = [bank[4], bank[5]]
        v_bank = bank[5][:, 2 * P:]
        shared_bank = [bank[6], bank[7]]

        d_const, d_ctx, d_wk, d_wv, d_wq, d_wo, d_bk, d_bq, d_bv, d_bo, d_gate = (
            sem("d_" + n) for n in ("const", "ctx", "wk", "wv", "wq", "wo", "bk", "bq", "bv", "bo", "gate"))
        d_x = [sem(f"d_x{i}") for i in range(XBUF)]
        d_x1 = [sem(f"d_x1{i}") for i in range(XBUF)]
        d_xn2 = sem("d_xn2")
        d_raw = [sem(f"d_raw{i}") for i in range(2)]
        d_raw2 = [sem(f"d_raw2{i}") for i in range(W2BUF)]
        p_w2lo, a_w2hi = sem("p_w2lo"), sem("a_w2hi")
        p_init, p_xb, p_wlo = (sem("p_" + n) for n in ("init", "xb", "wlo"))
        p_kblock, p_klo, p_wqo, v_bo, v_bvw, v_ctxT, t_bo, a_wq, a_wo = (
            sem(n) for n in ("p_kblock", "p_klo", "p_wqo", "v_bo", "v_bvw", "v_ctxT", "t_bo", "a_wq", "a_wo"))
        p_own, p_nr1, p_nr2, p_xnT, p_q = (sem("p_" + n) for n in ("own", "nr1", "nr2", "xnT", "q"))
        a_xn, a_xn2, a_xnTf, a_qf = (sem("a_" + n) for n in ("xn", "xn2", "xnTf", "qf"))
        v_bn1, v_bn2, v_max, v_recip, v_ones = (sem("v_" + n) for n in ("bn1", "bn2", "max", "recip", "ones"))
        t_ctx, t_k, t_v = (sem("t_" + n) for n in ("ctx", "k", "v"))
        t_xnT, t_q, t_score, t_probT, t_pv, t_attnT, t_wo, t_xn2T, t_logit = (
            sem("t_" + n) for n in ("xnT", "q", "score", "probT", "pv", "attnT", "wo", "xn2T", "logit"))
        a_tanh, a_ctxT, a_kT, a_khi = (sem("a_" + n) for n in ("tanh", "ctxT", "kT", "khi"))
        a_xnT, a_q, a_exp, a_probT, a_attnT, a_xn2T, a_whi = (
            sem("a_" + n) for n in ("xnT", "q", "exp", "probT", "attnT", "xn2T", "whi"))
        v_init, v_kblock, v_klo, v_vals, v_var1, v_sub, v_attn, v_attnT = (
            sem("v_" + n) for n in ("init", "kblock", "klo", "vals", "var1", "sub", "attn", "attnT"))
        v_x1, v_var2, v_logit, v_own = (sem("v_" + n) for n in ("x1", "var2", "logit", "own"))
        a_prob8 = sem("a_prob8")
        v_tile, v_gather, v_lists, v_route, v_places = (
            sem("v_" + n) for n in ("tile", "gather", "lists", "route", "places"))
        d_cst2 = sem("d_cst2")
        v_counters = sem("v_counters")
        t_rank, t_list = sem("t_rank"), sem("t_list")
        d_x1all = sem("d_x1all")
        d_xg = [sem(f"d_xg{i}") for i in range(XG)]
        d_ys = [sem(f"d_ys{i}") for i in range(2)]
        d_yin = [sem(f"d_yin{i}") for i in range(NT // CT)]
        d_out = sem("d_out")
        t_xgT, t_h, t_hT, t_y = (sem("t_" + n) for n in ("xgT", "h", "hT", "y"))
        a_xgT, a_relu, a_hT, a_y = (sem("a_" + n) for n in ("xgT", "relu", "hT", "y"))
        v_xgT, v_hsq, v_hT, v_out = (sem("v_" + n) for n in ("xgT", "hsq", "hT", "out"))

        SLOTS = range(-9, UNITS + 14)
        UB = UNITS // B
        EARLY, LATE = SLOTS[0] + 1, -4

        def tile_at(s, lag):
            t, odd = divmod(s - lag, 2)
            return t if not odd and 0 <= t < NT else None

        def group_at(s, lead):
            g, off = divmod(s + lead, 2 * GT)
            return g if not off and 0 <= g < NG else None

        attnT_tile = lambda s: tile_at(s, 3)
        wo_tile = lambda s: tile_at(s, 4)
        norm2_stats = lambda s: tile_at(s, 5)
        norm2_apply = lambda s: tile_at(s, 6)
        xn2T_tile = lambda s: tile_at(s, 7)
        logit_tile = lambda s: tile_at(s, 8)
        norm1_stats = lambda s: group_at(s, 9)
        norm1_apply = lambda s: group_at(s, 8)
        xnT_group = lambda s: group_at(s, 7)
        q_group = lambda s: group_at(s, 5)
        count_group = lambda s: group_at(s, -14)

        def value_step(s):
            for b in range(B):
                at_slots = [-7, -6, -4, -2, -1] if b == 0 else [UB * b - k for k in (15, 11, 7, 4, 3)]
                if s in at_slots:
                    return b * KC + at_slots.index(s)

        def key_step(s):
            for b in range(B):
                for c in range(DC):
                    if s == (c - 5 if b == 0 else UB * b - 12 + 4 * c):
                        return b, c

        def key_split(s):
            step = key_step(s)
            if step and step[0] == 0:
                return step
            step = key_step(s - 1)
            return step if step and step[0] else None

        def weight_piece(s):
            return s // 8 if s % 8 == 2 and 0 <= s // 8 < E else None

        def unit(u):
            return u if 0 <= u < UNITS else None

        def shared_steps(s):
            steps = (("xn2T", xn2T_tile(s)), ("logit", logit_tile(s)), ("count", count_group(s)),
                     ("attnT", attnT_tile(s)), ("wo", wo_tile(s)), ("xnT", xnT_group(s)), ("q", q_group(s)),
                     ("value", value_step(s)))
            return [step for step in steps if step[1] is not None]

        shared_order = [step for s in SLOTS for step in shared_steps(s)]
        shared_place = {step: shared_bank[n % 2] for n, step in enumerate(shared_order)}
        drained_by = {"xnT": a_xnTf, "q": a_qf, "attnT": v_attnT, "wo": v_x1, "xn2T": a_xn2T,
                      "logit": v_logit, "value": v_vals}

        first_steps = ["best0", "equal0", "lowest0", "key0", "pick0"]
        second_steps = ["masked", "best1", "equal1", "lowest1", "key1", "pick1", "both"]
        place_steps = [f"{what}{i}" for i in range(GT) for what in ("place", "count")]
        rank_steps = ["placed", "rank"]

        def route_plan(s):
            plan = []
            for lag, names in ((11, first_steps), (12, second_steps[:4]), (13, second_steps[4:]),
                               (14, [None, None] + place_steps), (17, rank_steps)):
                g = group_at(s, -lag)
                if g is not None:
                    plan += [name and (name, g) for name in names]
            return plan

        route_order = [step for s in SLOTS for step in route_plan(s) if step]
        routed_at = {step: n + 2 for n, step in enumerate(route_order)}
        ROUTED = 1 + len(route_order)
        x1_stores = [GT * len(range(i, NG, XBUF)) for i in range(XBUF)]

        def part_of(w, e):
            return w[:, e * EW:(e + 1) * EW]

        def key_block(b, c):
            return (kT[:, c, b * KEYS:(b + 1) * KEYS].unsqueeze(1).broadcast_to([P, UH, KEYS]),
                    C("kmask").unsqueeze(2).broadcast_to([P, UH, KEYS]))

        def ctx_copies(c):
            return (ctxT[:, c, :, :].rearrange("p b (r k) -> p b r k", k=KEYS),
                    bank[c][:, 0:B * KEYS].rearrange("p (b k) -> p b k", k=KEYS).unsqueeze(2).broadcast_to([P, B, 3, KEYS]))

        block = ctx.enter_context(nc.Block())

        @block.sync
        def _(sp):
            sp.dma_start(cst[:, :], consts[:, 0:at["iota"][0]]).then_inc(d_const, 16)
            sp.dma_start(wk_sb[:, :, :], wk.rearrange("(c p) n -> p c n", p=P)).then_inc(d_wk, 16)

            def load_x(g):
                if g >= XBUF:
                    sp.wait_ge(d_x1[g % XBUF], 16 * GT * (g // XBUF))
                    sp.wait_ge(a_xn2, GT * (g - XBUF + 1))
                sp.dma_start(xs[g % XBUF][:, :, :], x_rows[:, GT * g:GT * g + GT, :]).then_inc(d_x[g % XBUF], 16)

            load_x(0)
            sp.dma_start(bo_sb[:, :], bo.partition_broadcast(P)).then_inc(d_bo, 16)
            sp.dma_start(wq_sb[:, :, :], wq.rearrange("(c p) n -> p c n", p=P)).then_inc(d_wq, 16)
            for c in range(DC):
                sp.dma_start(bq_sb[:, c:c + 1], bq[c * P:(c + 1) * P].unsqueeze(1)).then_inc(d_bq, 16)
            load_x(1)
            sp.dma_start(wo_sb[:, :, :], wo.rearrange("(c p) n -> p c n", p=P)).then_inc(d_wo, 16)
            sp.dma_start(wg_sb[:, :, :], wg.rearrange("(c p) n -> p c n", p=P)).then_inc(d_wo, 16)
            for g in range(2, XBUF):
                load_x(g)

            def load_w1(k):
                if k >= 2:
                    sp.wait_ge(p_wlo, k - 1)
                sp.dma_start(raw[k % 2][:, :].rearrange("p (c n) -> p c n", c=DC),
                             w1[k].rearrange("(c p) n -> p c n", p=P)).then_inc(d_raw[k % 2], 16)

            load_w1(0)
            load_w1(1)
            for s in SLOTS:
                k = weight_piece(s - 2)
                if k is not None and k + 2 < E:
                    load_w1(k + 2)
                t = wo_tile(s)
                if t is not None:
                    sp.wait_ge(v_x1, t + 1)
                    sp.dma_start(x1_rows[:, t, :], xs[t // GT % XBUF][:, t % GT, :]).then_inc(d_x1[t // GT % XBUF], 16)
                t = norm2_apply(s)
                if t is not None:
                    sp.wait_ge(a_xn2, t + 1)
                    sp.dma_start(xn2_dram[t * P:(t + 1) * P, :], xn2[:, :]).then_inc(d_xn2, 16)
                    if t % GT == GT - 1 and t // GT + XBUF < NG:
                        load_x(t // GT + XBUF)
            def load_w2(k):
                if k >= W2BUF:
                    sp.wait_ge(p_w2lo, k - W2BUF + 1)
                sp.dma_start(raw2[k % W2BUF][:, :].rearrange("p (c n) -> p c n", c=HC),
                             w2[k].rearrange("(c p) n -> p c n", p=P)).then_inc(d_raw2[k % W2BUF], 16)

            sp.wait_ge(p_wlo, E)
            for k in range(2):
                load_w2(k)
            sp.wait_ge(v_logit, NT)
            sp.wait_ge(d_xn2, 16 * NT)
            for i in range(XBUF):
                sp.wait_ge(d_x1[i], 16 * x1_stores[i])
            sp.dma_start(cst2[:, :], consts[:, at["iota"][0]:]).then_inc(d_cst2, 16)
            for k in range(2, E):
                load_w2(k)
            sp.wait_ge(p_w2lo, E)
            sp.wait_ge(v_places, 1)
            for i in range(NT // CT):
                sp.wait_ge(t_y, 4 * i + 2)
                sp.dma_start(x1_all[:, i * CT:(i + 1) * CT, :], x1_rows[:, i * CT:(i + 1) * CT, :]).then_inc(d_x1all, 16)
            for i in range(2):
                sp.wait_ge(d_ys[i], 16 * len(range(i, NJ, 2)))
            for c in range(NT // CT):
                sp.dma_start(y_in[c], y_rows[:, c * CT:(c + 1) * CT, :, :]).then_inc(d_yin[c], 16)
            for c in range(NT // CT):
                sp.wait_ge(v_out, c + 1)
                sp.dma_start(out_rows[:, c * CT:(c + 1) * CT, :], x1_all[:, c * CT:(c + 1) * CT, :]).then_inc(d_out, 16)
            sp.wait_ge(d_out, 16 * (NT // CT))

        @block.gpsimd
        def _(pool):
            pool.memset(counters[:, 1, :], 1.0).then_inc(p_init, 1)
            pool.memset(exponent[:, :], -0.5).then_inc(p_init, 1)
            for c in range(DC):
                pool.dma_start(bk_sb[:, c:c + 1], bk[c * P:(c + 1) * P].unsqueeze(1)).then_inc(d_bk, 16)
            for c in range(DC):
                pool.dma_start(bv_sb[:, c:c + 1], bv[c * P:(c + 1) * P].unsqueeze(1)).then_inc(d_bv, 16)
            pool.memset(vals[:, B // 2:, :, :, :], 0.0).then_inc(p_init, 1)
            pool.wait_ge(p_init, 2)
            own = [0]

            def link(ins):
                own[0] += 1
                ins.then_inc(p_own, 1)
                pool.wait_ge(p_own, own[0])

            def scales(mv, ve, rs, nm, nr, done):
                pool.tensor_scalar(nm, mv[:, :, 0], -1.0, None, ALU.mult)
                link(pool.tensor_scalar(ve, mv[:, :, 1], EPS, None, ALU.add))
                link(pool.tensor_tensor(rs, ve, exponent[:, 0:ve.shape[1]], ALU.pow))
                pool.tensor_tensor(nr, nm, rs, ALU.mult).then_inc(done, 1)

            for s in SLOTS:
                t = norm2_stats(s)
                if t is not None:
                    pool.wait_ge(v_var2, t + 1)
                    pool.wait_ge(a_xn2, t)
                    scales(mv2[:, :].unsqueeze(1), ve2[:, :], rs2[:, :], nm2[:, :], nr2[:, :], p_nr2)
                g = norm1_stats(s)
                if g is not None:
                    pool.wait_ge(v_var1, g + 1)
                    pool.wait_ge(a_xn, g)
                    scales(mv1[:, :, :], ve1[:, :], rs1[:, :], nm1[:, :], nr1[:, :], p_nr1)
                step = key_split(s)
                if step and step[0]:
                    b, c = step
                    n = DC * (b - 1) + c
                    pool.wait_ge(v_klo, DC)
                    pool.wait_ge(a_khi, DC + n + 1)
                    pool.tensor_tensor(klo[b % 2][:, c, :], kblock[:, :, :].rearrange("p h k -> p (h k)"),
                                       khi[b % 2][:, c, :].bitcast(F32), ALU.subtract).then_inc(p_klo, 1)
                step = key_step(s)
                if step and step[0]:
                    b, c = step
                    pool.wait_ge(p_klo, DC * (b - 1) + c)
                    pool.wait_ge(v_klo, DC)
                    pool.tensor_tensor(kblock[:, :, :], *key_block(b, c), ALU.mult).then_inc(p_kblock, 1)
                if s == EARLY:
                    pool.wait_ge(a_wq, 1)
                    pool.tensor_tensor(wqlo[:, :, :], wq_sb[:, :, :], wqhi[:, :, :].bitcast(F32), ALU.subtract).then_inc(p_wqo, 1)
                g = xnT_group(s - 1)
                if g is not None:
                    pool.wait_ge(a_xnT, g + 1)
                    pool.tensor_tensor(xnTlo[:, :, :], xnT[:, :, :], xnThi[:, :, :].bitcast(F32),
                                       ALU.subtract).then_inc(p_xnT, 1)
                g = q_group(s - 1)
                if g is not None:
                    pool.wait_ge(a_q, g + 1)
                    pool.tensor_tensor(qTlo[g % 2][:, :, :], qT[:, :, :], qThi[g % 2][:, :, :].bitcast(F32),
                                       ALU.subtract).then_inc(p_q, 1)
                if s == LATE:
                    pool.wait_ge(a_wo, 1)
                    pool.tensor_tensor(wolo[:, :, :], wo_sb[:, :, :], wohi[:, :, :].bitcast(F32), ALU.subtract).then_inc(p_wqo, 1)
                g = norm1_apply(s - 3)
                if g is not None:
                    pool.wait_ge(a_xn, g + 1)
                    pool.wait_ge(v_bo, 1)
                    bo_b = bo_sb[:, :].unsqueeze(1).broadcast_to([P, GT, D])
                    pool.tensor_tensor(xs[g % XBUF][:, :, :], xs[g % XBUF][:, :, :], bo_b, ALU.add).then_inc(p_xb, 1)
                k = weight_piece(s)
                if k is not None:
                    pool.wait_ge(a_whi, k + 1)
                    pool.tensor_tensor(part_of(w1lo, k), raw[k % 2][:, :], part_of(w1hi, k).bitcast(F32),
                                       ALU.subtract).then_inc(p_wlo, 1)
            pool.wait_ge(v_logit, NT)
            pool.wait_ge(d_xn2, 16 * NT)
            for i in range(XBUF):
                pool.wait_ge(d_x1[i], 16 * x1_stores[i])
            for k in range(E):
                pool.wait_ge(a_w2hi, k + 1)
                pool.tensor_tensor(part_of(w2lo, k), raw2[k % W2BUF][:, :], part_of(w2hi, k).bitcast(F32),
                                   ALU.subtract).then_inc(p_w2lo, 1)
            pool.wait_ge(v_gather, 1)

            def gather(j):
                if j >= XG:
                    pool.wait_ge(t_xgT, j - XG + 1)
                pool.indirect_dma_start(xg[j % XG][:, :], None, xn2_dram[:, :],
                                        bass.IndirectOffsetOnAxis(ap=gather_at[:, j:j + 1], axis=0)).then_inc(d_xg[j % XG], 16)

            for j in range(XG - 1):
                gather(j)
            for j in range(NJ):
                if j + XG - 1 < NJ:
                    gather(j + XG - 1)
                pool.wait_ge(a_y, j + 1)
                pool.wait_ge(v_lists, 1)
                pool.indirect_dma_start(y_dram[:, :], bass.IndirectOffsetOnAxis(ap=scatter_at[:, j:j + 1], axis=0),
                                        y_sb[j % 2][:, :], None).then_inc(d_ys[j % 2], 16)

        @block.scalar
        def _(act):
            act.dma_start(ctx_sb[:, :, :], ctx_in.rearrange("b k d -> k b d")).then_inc(d_ctx, 16)
            act.dma_start(wv_sb[:, :, :], wv.rearrange("(c p) n -> p c n", p=P)).then_inc(d_wv, 16)
            act.dma_start(gates[:, 0:1], g_xattn.partition_broadcast(P)).then_inc(d_gate, 16)
            act.dma_start(gates[:, 1:2], g_ffn.partition_broadcast(P)).then_inc(d_gate, 16)
            act.wait_ge(t_ctx, 1)
            act.activation(*ctx_copies(0), ACT.Copy).then_inc(a_ctxT, 1)
            act.wait_ge(d_wq, 16)
            act.activation(wqhi[:, :, :], wq_sb[:, :, :], ACT.Copy).then_inc(a_wq, 1)
            act.wait_ge(d_bq, 16 * DC)

            for s in SLOTS:
                u = unit(s - 1)
                if u is not None:
                    if u >= 2:
                        act.wait_ge(t_pv, u - 1)
                    act.wait_ge(t_probT, 2 * u + 1)
                    act.activation(probT[u % 2][:, 0:3, :].rearrange("p c n -> p (c n)"), t_bank[0][:, 0:3 * P],
                                   ACT.Copy).then_inc(a_probT, 1)
                    act.wait_ge(t_probT, 2 * u + 2)
                    act.activation(probT[u % 2][:, 3:KC, :].rearrange("p c n -> p (c n)"), t_bank[1][:, 0:(KC - 3) * P],
                                   ACT.Copy).then_inc(a_probT, 1)
                g = xnT_group(s - 1)
                if g is not None:
                    act.wait_ge(a_xnTf, g + 1)
                    act.wait_ge(t_q, g)
                    act.activation(xnThi[:, :, :], xnT[:, :, :], ACT.Copy).then_inc(a_xnT, 1)
                g = q_group(s - 1)
                if g is not None:
                    act.wait_ge(a_qf, g + 1)
                    if g >= 2:
                        act.wait_ge(t_score, 2 * GT * (g - 1))
                    act.activation(qThi[g % 2][:, :, :], qT[:, :, :], ACT.Copy).then_inc(a_q, 1)
                t = norm2_apply(s)
                if t is not None:
                    act.wait_ge(p_nr2, t + 1)
                    act.wait_ge(d_xn2, 16 * t)
                    act.wait_ge(t_xn2T, t)
                    act.activation(xn2[:, :], xs[t // GT % XBUF][:, t % GT, :], ACT.Identity,
                                   bias=nr2[:, 0:1], scale=rs2[:, 0:1]).then_inc(a_xn2, 1)
                t = xn2T_tile(s)
                if t is not None:
                    act.wait_ge(t_xn2T, t + 1)
                    act.wait_ge(t_logit, t)
                    act.activation(xn2T[:, :, :], shared_place["xn2T", t][:, 0:D].rearrange("p (c n) -> p c n", n=P),
                                   ACT.Copy).then_inc(a_xn2T, 1)
                u = unit(s + 1)
                if u is not None:
                    act.wait_ge(v_sub, u + 1)
                    act.activation(prob[u % 2][:, 0:UC], prob[u % 2][:, 0:UC], ACT.Exp,
                                   scale=DH ** -0.5).then_inc(a_exp, 1)
                t = attnT_tile(s)
                if t is not None:
                    act.wait_ge(t_attnT, t + 1)
                    act.wait_ge(t_wo, t)
                    act.activation(attnThi[:, :, :], shared_place["attnT", t][:, 0:D].rearrange("p (c n) -> p c n", n=P),
                                   ACT.Copy).then_inc(a_attnT, 1)
                g = xnT_group(s)
                if g is not None:
                    act.wait_ge(t_xnT, g + 1)
                    act.wait_ge(p_xnT, g)
                    act.activation(xnT[:, :, :].rearrange("p c n -> p (c n)"), shared_place["xnT", g],
                                   ACT.Copy).then_inc(a_xnTf, 1)
                g = q_group(s)
                if g is not None:
                    act.wait_ge(t_q, g + 1)
                    act.wait_ge(p_q, g)
                    for c in range(DC):
                        ins = act.activation(qT[:, c, :], shared_place["q", g][:, c * GT * P:(c + 1) * GT * P],
                                             ACT.Identity, bias=bq_sb[:, c:c + 1])
                    ins.then_inc(a_qf, 1)
                g = norm1_apply(s)
                if g is not None:
                    act.wait_ge(p_nr1, g + 1)
                    act.wait_ge(d_x[g % XBUF], 16 * (g // XBUF + 1))
                    act.wait_ge(t_xnT, g)
                    for i in range(GT):
                        ins = act.activation(xn[:, i, :], xs[g % XBUF][:, i, :], ACT.Identity,
                                             bias=nr1[:, i:i + 1], scale=rs1[:, i:i + 1])
                    ins.then_inc(a_xn, 1)
                step = key_split(s)
                if step:
                    b, c = step
                    n = DC * b + c
                    if b:
                        act.wait_ge(p_kblock, n - DC + 1)
                    else:
                        act.wait_ge(v_kblock, n + 1)
                    act.activation(khi[b % 2][:, c, :], kblock[:, :, :].rearrange("p h k -> p (h k)"),
                                   ACT.Copy).then_inc(a_khi, 1)
                if s == EARLY:
                    act.wait_ge(d_bk, 16 * DC)
                    for c in range(DC):
                        act.wait_ge(t_k, c + 1)
                        act.activation(kT[:, c, :], bank[2 + c][:, 0:B * KEYS], ACT.Identity,
                                       bias=bk_sb[:, c:c + 1]).then_inc(a_kT, 1)
                    act.wait_ge(d_wo, 32)
                    act.activation(wohi[:, :, :], wo_sb[:, :, :], ACT.Copy).then_inc(a_wo, 1)
                    act.wait_ge(d_gate, 32)
                    act.activation(tg[:, :], gates[:, :], ACT.Tanh).then_inc(a_tanh, 1)
                k = weight_piece(s)
                if k is not None:
                    act.wait_ge(d_raw[k % 2], 16 * (k // 2 + 1))
                    act.activation(part_of(w1hi, k), raw[k % 2][:, :], ACT.Copy).then_inc(a_whi, 1)
            for k in range(E):
                act.wait_ge(d_raw2[k % W2BUF], 16 * (k // W2BUF + 1))
                act.activation(part_of(w2hi, k), raw2[k % W2BUF][:, :], ACT.Copy).then_inc(a_w2hi, 1)
            def store_y(j):
                act.wait_ge(t_y, j + 1)
                if j >= 2:
                    act.wait_ge(d_ys[j % 2], 16 * (j // 2))
                act.activation(y_sb[j % 2][:, :], bank[6 + j % 2][:, 0:D], ACT.Copy).then_inc(a_y, 1)

            for j in range(-3, NJ + 1):
                if j == 3:
                    act.wait_ge(v_route, ROUTED + 1)
                    act.activation(weight8[:, :, :], weight8[:, :, :], ACT.Exp).then_inc(a_prob8, 1)
                if 0 <= j - 2:
                    store_y(j - 2)
                if 0 <= j < NJ:
                    act.wait_ge(t_hT, j + 1)
                    if j >= 2:
                        act.wait_ge(t_y, j - 1)
                    act.activation(hThi[j % 2][:, :, :].rearrange("p c n -> p (c n)"), bank[2 + j % 2][:, :],
                                   ACT.Copy).then_inc(a_hT, 1)
                if j + 3 < NJ:
                    i = j + 3
                    act.wait_ge(t_xgT, i + 1)
                    if i >= 2:
                        act.wait_ge(t_h, i - 1)
                    act.activation(xgThi[i % 2][:, :, :].rearrange("p c n -> p (c n)"), bank[4 + i % 2][:, 0:D],
                                   ACT.Copy).then_inc(a_xgT, 1)
                if 0 <= j + 2 < NJ:
                    i = j + 2
                    act.wait_ge(t_h, i + 1)
                    act.wait_ge(v_hsq, i)
                    act.activation(hrelu[:, :], bank[i % 2][:, :], ACT.Relu).then_inc(a_relu, 1)
            store_y(NJ - 1)

        @block.tensor
        def _(pe):
            def three_pass(dst, hi_l, lo_l, hi_r, lo_r, n):
                passes = [(l, r) for l, r in ((hi_l, hi_r), (hi_l, lo_r), (lo_l, hi_r))]
                for k in range(n):
                    for i, (l, r) in enumerate(passes):
                        mm = pe.matmul(dst, l(k), r(k), start=(k == 0 and i == 0), stop=(k == n - 1 and i == 2))
                return mm

            pe.wait_ge(d_const, 16)
            pe.wait_ge(d_ctx, 16)
            for c in range(DC):
                for b in range(B):
                    mm = pe.transpose(bank[c][:, b * KEYS:(b + 1) * KEYS], ctx_sb[:, b, c * P:(c + 1) * P],
                                      ident[0:KEYS, 0:KEYS])
                mm.then_inc(t_ctx, 1)
            pe.wait_ge(d_wk, 16)
            pe.wait_ge(a_ctxT, 1)
            pe.wait_ge(v_ctxT, 1)
            for c in range(DC):
                for d in range(DC):
                    mm = pe.matmul(bank[2 + c][:, 0:B * KEYS], wk_sb[:, d, c * P:(c + 1) * P],
                                   ctxT[:, d, :, 0:KEYS], start=(d == 0), stop=(d == DC - 1))
                mm.then_inc(t_k, 1)
            pe.wait_ge(v_bvw, 1)
            pe.wait_ge(d_wo, 32)
            for d in range(DC):
                mm = pe.matmul(bank[4][:, 0:D], bv_wide[:, d, :], wo_sb[:, d, :], start=(d == 0), stop=(d == DC - 1))
            mm.then_inc(t_bo, 1)
            pe.wait_ge(d_wv, 16)

            shared_n = [0]

            def take_shared():
                if shared_n[0] >= 2:
                    what, n = shared_order[shared_n[0] - 2]
                    if what == "count":
                        pe.wait_ge(v_route, routed_at[f"count{GT - 1}", n])
                    else:
                        pe.wait_ge(drained_by[what], n + 1)
                shared_n[0] += 1

            for s in SLOTS:
                u = unit(s + 2)
                if u is not None:
                    t, c = divmod(u, 2)
                    g = t // GT
                    if u % (2 * GT) == 0:
                        pe.wait_ge(p_q, g + 1)
                    if u % UB < DC:
                        if g < GPB:
                            pe.wait_ge(v_klo, c + 1)
                        else:
                            pe.wait_ge(p_klo, DC * (g // GPB - 1) + c + 1)
                    if u >= 2:
                        pe.wait_ge(v_sub, u - 1)
                    qs = slice(t % GT * P, t % GT * P + P)
                    b = g // GPB
                    for j in range(2):
                        js = slice(j * QC, (j + 1) * QC)
                        mm = three_pass(pair[u % 2][:, j, 0:QC],
                                        lambda k: qThi[g % 2][:, c, qs], lambda k: qTlo[g % 2][:, c, qs],
                                        lambda k: khi[b % 2][:, c, js], lambda k: klo[b % 2][:, c, js], 1)
                    mm.then_inc(t_score, 1)
                t = xn2T_tile(s)
                if t is not None:
                    take_shared()
                    pe.wait_ge(a_xn2, t + 1)
                    for c in range(DC):
                        mm = pe.transpose(shared_place["xn2T", t][:, c * P:(c + 1) * P],
                                          xn2[:, c * P:(c + 1) * P], ident)
                    mm.then_inc(t_xn2T, 1)
                t = logit_tile(s)
                if t is not None:
                    take_shared()
                    pe.wait_ge(a_xn2T, t + 1)
                    for c in range(DC):
                        mm = pe.matmul(shared_place["logit", t][:, 0:E], xn2T[:, c, :], wg_sb[:, c, :],
                                       start=(c == 0), stop=(c == DC - 1))
                    mm.then_inc(t_logit, 1)
                g = count_group(s)
                if g is not None:
                    take_shared()
                    pe.wait_ge(v_route, routed_at["both", g])
                    if g == 0:
                        pe.wait_ge(v_counters, 1)
                        pe.wait_ge(p_init, 1)
                    pickf = both[:, :, :].rearrange("p t e -> p (t e)")
                    for i, rows_of in enumerate((counters[:, 0, :], counters[:, 1, :])):
                        mm = pe.matmul(shared_place["count", g][:, i * GT * E:(i + 1) * GT * E], rows_of, pickf,
                                       start=True, stop=True)
                    mm.then_inc(t_rank, 1)
                u = unit(s - 1)
                if u is not None:
                    t, c = divmod(u, 2)
                    b = t // (NT // B)
                    pe.wait_ge(a_probT, 2 * u + 2)
                    if u % UB == 0:
                        pe.wait_ge(v_vals, (b + 1) * KC)
                        pe.wait_ge(v_ones, 1)
                    for i in range(KC):
                        mm = pe.matmul(v_bank[:, 0:UH * VW], probT[u % 2][:, i, :], vals[:, b, c, i, :],
                                       start=(i == 0), stop=(i == KC - 1))
                    mm.then_inc(t_pv, 1)
                t = attnT_tile(s)
                if t is not None:
                    take_shared()
                    pe.wait_ge(v_attn, 2 * t + 2)
                    for c in range(DC):
                        mm = pe.transpose(shared_place["attnT", t][:, c * P:(c + 1) * P], attn[:, c * P:(c + 1) * P], ident)
                    mm.then_inc(t_attnT, 1)
                t = wo_tile(s)
                if t is not None:
                    take_shared()
                    pe.wait_ge(v_attnT, t + 1)
                    pe.wait_ge(p_wqo, 2)
                    mm = three_pass(shared_place["wo", t][:, 0:D], lambda k: attnThi[:, k, :], lambda k: attnTlo[:, k, :],
                                    lambda k: wohi[:, k, :], lambda k: wolo[:, k, :], DC)
                    mm.then_inc(t_wo, 1)
                g = xnT_group(s)
                if g is not None:
                    take_shared()
                    pe.wait_ge(a_xn, g + 1)
                    for c in range(DC):
                        for i in range(GT):
                            mm = pe.transpose(shared_place["xnT", g][:, (c * GT + i) * P:(c * GT + i + 1) * P],
                                              xn[:, i, c * P:(c + 1) * P], ident)
                    mm.then_inc(t_xnT, 1)
                g = q_group(s)
                if g is not None:
                    take_shared()
                    pe.wait_ge(p_xnT, g + 1)
                    pe.wait_ge(p_wqo, 1)
                    for c in range(DC):
                        cs = slice(c * P, (c + 1) * P)
                        mm = three_pass(shared_place["q", g][:, c * GT * P:(c + 1) * GT * P],
                                        lambda k: wqhi[:, k, cs], lambda k: wqlo[:, k, cs],
                                        lambda k: xnThi[:, k, :], lambda k: xnTlo[:, k, :], DC)
                    mm.then_inc(t_q, 1)
                u = unit(s)
                if u is not None:
                    pe.wait_ge(a_exp, u + 1)
                    if u == 0:
                        pe.wait_ge(v_bo, 1)
                    for i in range(KC):
                        tb = t_bank[i // 3]
                        if i == 3 and u:
                            pe.wait_ge(v_attn, u)
                        mm = pe.transpose(tb[:, (i % 3) * P:(i % 3 + 1) * P], prob[u % 2][:, i * P:(i + 1) * P], ident)
                        if i in (2, KC - 1):
                            mm.then_inc(t_probT, 1)
                n = value_step(s)
                if n is not None:
                    b, i = divmod(n, KC)
                    take_shared()
                    dst = shared_place["value", n][:, 0:2 * WIN * DH].rearrange("p (c n) -> p c n", c=2)
                    at0 = P * i % KEYS
                    for d in range(DC):
                        cols = wv_sb[:, d, :].rearrange("p (c h e) -> p c (h e)", c=2, e=DH)
                        mm = pe.matmul(dst, ctxT[:, d, b, at0:at0 + P], cols[:, :, HEAD0[i] * DH:(HEAD0[i] + WIN) * DH],
                                       start=(d == 0), stop=(d == DC - 1))
                    mm.then_inc(t_v, 1)

            for q in range(NC // PART):
                for i in range(PART):
                    n = q * PART + i
                    if i % TP == 0:
                        pe.wait_ge(v_tile, n // TP + 1)
                    mm = pe.matmul(bank[2 + n // NT][:, 0:NJE], onehot_row[q % 2][:, i, :], onehot_tile[q % 2][:, i, :],
                                   start=(n % NT == 0), stop=(n % NT == NT - 1))
                mm.then_inc(t_list, 1)

            pe.wait_ge(v_places, 1)
            pe.wait_ge(p_wlo, E)
            pe.wait_ge(p_w2lo, E)
            expert = [None] * NJ
            for j in range(-3, NJ + 1):
                if 0 <= j < NJ:
                    pe.wait_ge(v_hsq, j + 1)
                    if j >= 2:
                        pe.wait_ge(v_hT, j - 1)
                    for c in range(HC):
                        mm = pe.transpose(bank[2 + j % 2][:, c * P:(c + 1) * P], hsq[j % 2][:, c * P:(c + 1) * P], ident)
                    mm.then_inc(t_hT, 1)
                if j + 3 < NJ:
                    i = j + 3
                    pe.wait_ge(d_xg[i % XG], 16 * (i // XG + 1))
                    if i >= 2:
                        pe.wait_ge(v_xgT, i - 1)
                    for c in range(DC):
                        mm = pe.transpose(bank[4 + i % 2][:, c * P:(c + 1) * P], xg[i % XG][:, c * P:(c + 1) * P], ident)
                    mm.then_inc(t_xgT, 1)
                if 0 <= j + 2 < NJ:
                    i = j + 2
                    if i % RL == 0:
                        n = min(RL, NJ - i)
                        _, expert[i:i + n] = nc.values_load_multi_w_load_instructions(
                            expert_at[0:1, i:i + n], engines=(mybir.EngineType.PE,), min_val=0, max_val=(E - 1) * EW,
                            skip_runtime_bounds_check_because="it is EW times a count of at most E - 1 experts")
                    pe.wait_ge(v_xgT, i + 1)
                    if i >= 2:
                        pe.wait_ge(v_hsq, i - 1)
                    w = lambda part, k: part[:, bass.ds(expert[i] + k * H, H)]
                    mm = three_pass(bank[i % 2][:, :], lambda k: xgThi[i % 2][:, k, :], lambda k: xgTlo[i % 2][:, k, :],
                                    lambda k: w(w1hi, k), lambda k: w(w1lo, k), DC)
                    mm.then_inc(t_h, 1)
                if 0 <= j - 1:
                    i = j - 1
                    pe.wait_ge(v_hT, i + 1)
                    if i >= 2:
                        pe.wait_ge(a_y, i - 1)
                    w = lambda part, k: part[:, bass.ds(expert[i] + k * D, D)]
                    mm = three_pass(bank[6 + i % 2][:, 0:D], lambda k: hThi[i % 2][:, k, :], lambda k: hTlo[i % 2][:, k, :],
                                    lambda k: w(w2hi, k), lambda k: w(w2lo, k), HC)
                    mm.then_inc(t_y, 1)

        @block.vector
        def _(dve):
            own = [0]

            def link(ins):
                own[0] += 1
                ins.then_inc(v_own, 1)
                dve.wait_ge(v_own, own[0])

            for i in range(2):
                dve.memset(prob[i][:, UC:UPAD], 0.0).then_inc(v_init, 1)
            dve.memset(vals[:, 0:B // 2, :, :, :], 0.0).then_inc(v_init, 1)
            dve.wait_ge(d_const, 16)
            dve.wait_ge(t_ctx, 2)
            dve.tensor_copy(*ctx_copies(1)).then_inc(v_ctxT, 1)

            def route_step(name, g):
                ts = slice(g * GT, (g + 1) * GT)
                kind, i = (name[:-1], int(name[-1])) if name[-1].isdigit() else (name, 0)
                over_e = lambda a: a.unsqueeze(2).broadcast_to([P, GT, E])
                values = masked[:, :, :] if i else logits[:, ts, :]
                if kind == "best":
                    if i == 0:
                        dve.wait_ge(v_logit, GT * (g + 1))
                    return dve.tensor_reduce(best[:, i, ts], values, AX.X, ALU.max)
                if kind == "equal":
                    return dve.tensor_tensor(chosen[:, :, :], values, over_e(best[:, i, ts]), ALU.is_equal)
                if kind == "lowest":
                    return dve.tensor_tensor(chosen[:, :, :], chosen[:, :, :],
                                             C("lowest").unsqueeze(1).broadcast_to([P, GT, E]), ALU.mult)
                if kind == "key":
                    return dve.tensor_reduce(key[:, :], chosen[:, :, :], AX.X, ALU.max)
                if kind == "pick":
                    return dve.tensor_tensor(pick[:, i, ts, :], chosen[:, :, :], over_e(key[:, :]), ALU.is_equal)
                if kind == "masked":
                    return dve.scalar_tensor_tensor(out=masked[:, :, :], in0=pick[:, 0, ts, :], scalar=LOW,
                                                    in1=logits[:, ts, :], op0=ALU.mult, op1=ALU.add)
                if kind == "both":
                    dve.wait_ge(t_rank, g)
                    return dve.tensor_tensor(both[:, :, :], pick[:, 0, ts, :], pick[:, 1, ts, :], ALU.add)
                counts = shared_place["count", g][:, 0:2 * GT * E].rearrange("p (i t e) -> p i t e", i=2, e=E)
                if kind == "place":
                    dve.wait_ge(t_rank, g + 1)
                    return dve.tensor_tensor(place_te[:, i, :], counts[:, 0, i, :], count[:, :], ALU.add)
                if kind == "count":
                    return dve.tensor_tensor(count[:, :], counts[:, 1, i, :], count[:, :], ALU.add)
                if kind == "placed":
                    return dve.tensor_tensor(placed[:, :, :, :], pick[:, :, ts, :], place_te[:, :, :].unsqueeze(1)
                                             .broadcast_to([P, CHOICES, GT, E]), ALU.mult)
                if kind == "rank":
                    return dve.tensor_reduce(rank[:, :, ts], placed[:, :, :, :], AX.X, ALU.add)

            dve.memset(count[:, :], 0.0).then_inc(v_route, 1)
            dve.tensor_copy(counters[:, 0, :], C("before")).then_inc(v_counters, 1)

            for s in SLOTS:
                if s == EARLY:
                    dve.wait_ge(d_bv, 16 * DC)
                    dve.tensor_copy(bv_wide[:, :, :], bv_sb[:, :].unsqueeze(2).broadcast_to([P, DC, P])).then_inc(v_bvw, 1)
                    dve.wait_ge(d_bo, 16)
                    dve.wait_ge(t_bo, 1)
                    dve.wait_ge(a_tanh, 1)
                    link(dve.tensor_tensor(bo_sb[:, :], bank[4][:, 0:D], bo_sb[:, :], ALU.add))
                    dve.tensor_scalar(bo_sb[:, :], bo_sb[:, :], tg[:, 0:1], None, ALU.mult).then_inc(v_bo, 1)
                    dve.wait_ge(v_init, 3)
                    dve.wait_ge(p_init, 3)
                    for i in range(KC):
                        heads = vals[:, :, :, i, :].rearrange("p b c (h e) -> p (b c) h e", e=VW)
                        ins = dve.tensor_copy(heads[:, :, HEAD0[i]:HEAD0[i] + WIN, DH],
                                              C("vmask")[:, i * WIN:(i + 1) * WIN].unsqueeze(1).broadcast_to([P, 2 * B, WIN]))
                    ins.then_inc(v_ones, 1)
                plan = route_plan(s)

                def route_one():
                    if plan and plan[0]:
                        dve.wait_ge(v_route, routed_at[plan[0]] - 1)
                        route_step(*plan[0]).then_inc(v_route, 1)
                    if plan:
                        plan.pop(0)

                u1 = unit(s + 1)
                if u1 is not None:
                    dve.wait_ge(t_score, u1 + 1)
                    dve.wait_ge(v_sub, u1)
                    scores = pair[u1 % 2][:, :, 0:QC].rearrange("p j (h k) -> p j h k", k=KEYS)
                    dve.tensor_reduce(rowmax[:, :].rearrange("p (j h) -> p j h", j=2), scores, AX.X,
                                      ALU.max).then_inc(v_max, 1)
                route_one()
                t2 = norm2_stats(s)
                if t2 is not None:
                    dve.wait_ge(v_x1, t2 + 1)
                    dve.bn_stats(st2[:, :], xs[t2 // GT % XBUF][:, t2 % GT, :]).then_inc(v_bn2, 1)
                if u1 is not None:
                    dve.wait_ge(v_max, u1 + 1)
                    if u1 >= 2:
                        dve.wait_ge(t_probT, 2 * (u1 - 1))
                    dve.tensor_tensor(prob[u1 % 2][:, 0:UC].rearrange("p (j h k) -> p j h k", j=2, k=KEYS), scores,
                                      rowmax[:, :].rearrange("p (j h) -> p j h", j=2).unsqueeze(3)
                                      .broadcast_to([P, 2, QH, KEYS]), ALU.subtract).then_inc(v_sub, 1)
                if t2 is not None:
                    dve.wait_ge(v_bn2, t2 + 1)
                    dve.wait_ge(p_nr2, t2)
                    dve.bn_aggr(mv2[:, :], st2[:, :]).then_inc(v_var2, 1)
                route_one()
                t = logit_tile(s)
                if t is not None:
                    dve.wait_ge(t_logit, t + 1)
                    dve.tensor_copy(logits[:, t, :], shared_place["logit", t][:, 0:E]).then_inc(v_logit, 1)
                u = unit(s - 1)
                if u is not None:
                    t, c = divmod(u, 2)
                    dve.wait_ge(t_pv, u + 1)
                    dve.wait_ge(v_attn, u)
                    pv = v_bank[:, 0:UH * VW].rearrange("p (h e) -> p h e", e=VW)
                    dve.reciprocal(recip[:, :], pv[:, :, DH]).then_inc(v_recip, 1)
                route_one()
                g = norm1_stats(s)
                if g is not None:
                    dve.wait_ge(d_x[g % XBUF], 16 * (g // XBUF + 1))
                    dve.wait_ge(p_nr1, g)
                    dve.wait_ge(v_var1, g)
                    for i in range(GT):
                        ins = dve.bn_stats(st1[:, i, :], xs[g % XBUF][:, i, :])
                    ins.then_inc(v_bn1, 1)
                if u is not None:
                    dve.wait_ge(v_recip, u + 1)
                    if c == 0 and t:
                        dve.wait_ge(t_attnT, t)
                    dve.tensor_tensor(attn[:, c * P:(c + 1) * P].rearrange("p (h e) -> p h e", e=DH),
                                      pv[:, :, 0:DH], recip[:, :].unsqueeze(2).broadcast_to([P, UH, DH]),
                                      ALU.mult).then_inc(v_attn, 1)
                route_one()
                t = attnT_tile(s)
                if t is not None:
                    dve.wait_ge(a_attnT, t + 1)
                    dve.tensor_tensor(attnTlo[:, :, :], shared_place["attnT", t][:, 0:D].rearrange("p (c n) -> p c n", n=P),
                                      attnThi[:, :, :].bitcast(F32), ALU.subtract).then_inc(v_attnT, 1)
                if g is not None:
                    dve.wait_ge(v_bn1, g + 1)
                    for i in range(GT):
                        ins = dve.bn_aggr(mv1[:, i, :], st1[:, i, :])
                    ins.then_inc(v_var1, 1)
                t = wo_tile(s)
                if t is not None:
                    x1 = xs[t // GT % XBUF][:, t % GT, :]
                    dve.wait_ge(t_wo, t + 1)
                    dve.wait_ge(p_xb, t // GT + 1)
                    dve.scalar_tensor_tensor(out=x1, in0=shared_place["wo", t][:, 0:D], scalar=tg[:, 0:1], in1=x1,
                                             op0=ALU.mult, op1=ALU.add).then_inc(v_x1, 1)
                n = value_step(s)
                if n is not None:
                    b, i = divmod(n, KC)
                    dve.wait_ge(t_v, n + 1)
                    mask = C("vmask")[:, i * WIN:(i + 1) * WIN]
                    heads = vals[:, b, :, i, :].rearrange("p c (h e) -> p c h e", e=VW)
                    dve.tensor_tensor(heads[:, :, HEAD0[i]:HEAD0[i] + WIN, 0:DH],
                                      shared_place["value", n][:, 0:2 * WIN * DH].rearrange("p (c w e) -> p c w e", c=2, e=DH),
                                      mask.unsqueeze(1).unsqueeze(3).broadcast_to([P, 2, WIN, DH]), ALU.mult).then_inc(v_vals, 1)
                route_one()
                step = key_step(s)
                if step and step[0] == 0:
                    c = step[1]
                    dve.wait_ge(a_kT, c + 1)
                    dve.wait_ge(v_klo, c)
                    dve.tensor_tensor(kblock[:, :, :], *key_block(0, c), ALU.mult).then_inc(v_kblock, 1)
                    dve.wait_ge(a_khi, c + 1)
                    dve.tensor_tensor(klo[0][:, c, :], kblock[:, :, :].rearrange("p h k -> p (h k)"),
                                      khi[0][:, c, :].bitcast(F32), ALU.subtract).then_inc(v_klo, 1)
                while plan:
                    route_one()

            tt = lambda *a: link(dve.tensor_tensor(*a))
            ts = lambda *a: link(dve.tensor_scalar(*a))
            dve.wait_ge(v_route, ROUTED)
            dve.wait_ge(v_logit, NT)
            dve.wait_ge(p_wlo, E)
            dve.wait_ge(d_xn2, 16 * NT)
            for i in range(XBUF):
                dve.wait_ge(d_x1[i], 16 * x1_stores[i])
            dve.wait_ge(d_cst2, 16)
            def step(ins):
                own[0] += 1
                ins.then_inc(v_own, 1)
                return own[0]

            def rows_of_part(q):
                if q >= 2:
                    dve.wait_ge(t_list, q - 1)
                dve.tensor_tensor(onehot_row[q % 2][:, :, :],
                                  row_i[:, q * PART:(q + 1) * PART].unsqueeze(2).broadcast_to([P, PART, P]),
                                  C2("iota").unsqueeze(1).broadcast_to([P, PART, P]), ALU.is_equal)

            need0 = step(dve.tensor_scalar(need_i[0][:, :], count[:, :], float(P - 1), None, ALU.add))
            ranks = step(dve.tensor_copy(rank_i[:, :], rank[:, :, :].rearrange("p k t -> p (k t)")))
            dve.wait_ge(v_own, need0)
            need1 = step(dve.tensor_scalar(need_i[1][:, :], need_i[0][:, :], P.bit_length() - 1, None,
                                           ALU.logical_shift_right))
            dve.wait_ge(v_own, ranks)
            step(dve.tensor_scalar(row_i[:, :], rank_i[:, :], P - 1, None, ALU.bitwise_and))
            dve.wait_ge(v_own, need1)
            need2 = step(dve.tensor_copy(need[:, :], need_i[1][:, :]))
            tiles = step(dve.tensor_scalar(tile_i[:, :], rank_i[:, :], P.bit_length() - 1, None, ALU.logical_shift_right))
            dve.wait_ge(v_own, need2)
            summed = step(dve.tensor_tensor(sums[:, :, :], C2("upto").rearrange("p (n e) -> p n e", e=E),
                                            need[:, :].unsqueeze(1).broadcast_to([P, 2 * E, E]), ALU.mult))
            dve.wait_ge(v_own, tiles)
            rows_of_part(0)
            dve.wait_ge(v_own, summed)
            link(dve.tensor_reduce(bounds[:, :], sums[:, :, :], AX.X, ALU.add))
            picks = step(dve.tensor_tensor(picked[:, :, :], pick[:, :, :, :].rearrange("p k t e -> p (k t) e"),
                                           bounds[:, E:2 * E].unsqueeze(1).broadcast_to([P, NC, E]), ALU.mult))
            rows_of_part(1)
            dve.wait_ge(v_own, picks)
            link(dve.tensor_reduce(first_of[:, :], picked[:, :, :], AX.X, ALU.add))
            tt(tile_of[:, :], first_of[:, :], tile_i[:, :], ALU.add)
            def hits_of_part(q):
                if q >= 2:
                    dve.wait_ge(v_tile, (q - 1) * PART // TP)
                return step(dve.tensor_tensor(
                    hit[q % 2][:, :, :], tile_of[:, q * PART:(q + 1) * PART].unsqueeze(2).broadcast_to([P, PART, NJE]),
                    C2("iota")[:, 0:NJE].unsqueeze(1).broadcast_to([P, PART, NJE]), ALU.is_equal))

            made = [hits_of_part(0), hits_of_part(1)]
            for q in range(NC // PART):
                if q >= 2:
                    made.append(hits_of_part(q))
                    rows_of_part(q)
                dve.wait_ge(v_own, made[q])
                for i in range(0, PART, TP):
                    t = (q * PART + i) % NT
                    dve.tensor_tensor(onehot_tile[q % 2][:, i:i + TP, :], hit[q % 2][:, i:i + TP, :],
                                      C2("token")[:, t:t + TP].unsqueeze(2).broadcast_to([P, TP, NJE]),
                                      ALU.mult).then_inc(v_tile, 1)
            dve.wait_ge(t_list, NC // PART)
            dve.tensor_scalar(second[:, :], bank[3][:, 0:NJ], 0.0, None, ALU.is_gt)
            link(dve.tensor_copy(code0[:, :], bank[2][:, 0:NJ]))
            tt(code[:, :], code0[:, :], bank[3][:, 0:NJ], ALU.add)
            dve.tensor_scalar(gather_at[:, :], code[:, :], -1.0, 0.0, ALU.add, ALU.max).then_inc(v_gather, 1)
            dve.tensor_scalar(empty[:, :], code[:, :], 0.0, None, ALU.is_equal)
            link(dve.scalar_tensor_tensor(out=yrow[:, :], in0=code[:, :], scalar=float(CHOICES), in1=second[:, :],
                                          op0=ALU.mult, op1=ALU.add))
            tt(empty[:, :], empty[:, :], C2("spare"), ALU.mult)
            dve.scalar_tensor_tensor(out=scatter_at[:, :], in0=yrow[:, :], scalar=-float(CHOICES), in1=empty[:, :],
                                     op0=ALU.add, op1=ALU.add).then_inc(v_lists, 1)
            tt(ended[:, :, :], bounds[0:1, 0:E - 1].unsqueeze(1).broadcast_to([1, NJ, E - 1]),
               C2("iota")[0:1, 0:NJ].unsqueeze(2).broadcast_to([1, NJ, E - 1]), ALU.is_le)
            link(dve.tensor_reduce(ended_n[:, :], ended[:, :, :], AX.X, ALU.add))
            dve.tensor_scalar(expert_at[:, :], ended_n[:, :], float(EW), None, ALU.mult).then_inc(v_places, 1)

            over_e = lambda a: a.unsqueeze(2).broadcast_to([P, NT, E])

            def exp_sum():
                dve.wait_ge(a_prob8, 1)
                return dve.tensor_reduce(total[:, :], weight8[:, :, :], AX.X, ALU.add)

            weigh = {0: lambda: dve.tensor_tensor(weight8[:, :, :], logits[:, :, :], over_e(best[:, 0, :]), ALU.subtract),
                     4: exp_sum,
                     5: lambda: dve.reciprocal(total[:, :], total[:, :]),
                     6: lambda: dve.tensor_tensor(weight8[:, :, :], weight8[:, :, :], over_e(total[:, :]), ALU.mult),
                     7: lambda: dve.tensor_tensor(weighed[:, :, :, :], pick[:, :, :, :], weight8[:, :, :].unsqueeze(1)
                                                  .broadcast_to([P, CHOICES, NT, E]), ALU.mult),
                     8: lambda: dve.tensor_reduce(tile_w[:, :, :], weighed[:, :, :, :], AX.X, ALU.add),
                     9: lambda: dve.tensor_tensor(total[:, :], tile_w[:, 0, :], tile_w[:, 1, :], ALU.add),
                     10: lambda: dve.tensor_scalar(total[:, :], total[:, :], 1e-8, None, ALU.add),
                     11: lambda: dve.reciprocal(total[:, :], total[:, :]),
                     12: lambda: dve.tensor_tensor(tile_w[:, :, :], tile_w[:, :, :],
                                                   total[:, :].unsqueeze(1).broadcast_to([P, CHOICES, NT]), ALU.mult),
                     13: lambda: dve.tensor_scalar(tile_w[:, :, :], tile_w[:, :, :], tg[:, 1:2], None, ALU.mult)}
            for j in range(-3, NJ):
                if 0 <= j:
                    dve.wait_ge(a_hT, j + 1)
                    dve.tensor_tensor(hTlo[j % 2][:, :, :].rearrange("p c n -> p (c n)"), bank[2 + j % 2][:, :],
                                      hThi[j % 2][:, :, :].rearrange("p c n -> p (c n)").bitcast(F32),
                                      ALU.subtract).then_inc(v_hT, 1)
                if j + 3 < NJ:
                    i = j + 3
                    dve.wait_ge(a_xgT, i + 1)
                    dve.tensor_tensor(xgTlo[i % 2][:, :, :].rearrange("p c n -> p (c n)"), bank[4 + i % 2][:, 0:D],
                                      xgThi[i % 2][:, :, :].rearrange("p c n -> p (c n)").bitcast(F32),
                                      ALU.subtract).then_inc(v_xgT, 1)
                if 0 <= j + 2 < NJ:
                    i = j + 2
                    dve.wait_ge(a_relu, i + 1)
                    if i >= 2:
                        dve.wait_ge(t_hT, i - 1)
                    dve.tensor_tensor(hsq[i % 2][:, :], bank[i % 2][:, :], hrelu[:, :], ALU.mult).then_inc(v_hsq, 1)
                if j in weigh:
                    dve.wait_ge(v_route, ROUTED + sorted(weigh).index(j))
                    weigh[j]().then_inc(v_route, 1)

            dve.wait_ge(d_x1all, 16 * (NT // CT))
            dve.wait_ge(v_route, ROUTED + len(weigh))
            for c in range(NT // CT):
                dve.wait_ge(d_yin[c], 16)
                for k in range(CHOICES):
                    for i in range(CT):
                        t = c * CT + i
                        ins = dve.scalar_tensor_tensor(out=x1_all[:, t, :], in0=y_in[c][:, i, k, :],
                                                       scalar=tile_w[:, k, t:t + 1], in1=x1_all[:, t, :],
                                                       op0=ALU.mult, op1=ALU.add)
                    if k < CHOICES - 1:
                        link(ins)
                ins.then_inc(v_out, 1)


_INS = ["x", "ctx_1024", "g_xattn", "g_ffn", "L0_xattn_Wq", "L0_xattn_Wk", "L0_xattn_Wv", "L0_xattn_Wo",
        "L0_xattn_bq", "L0_xattn_bk", "L0_xattn_bv", "L0_xattn_bo", "L0_ffn_Wg", "L0_ffn_W1", "L0_ffn_W2"]


def kernel(**inputs):
    import numpy as _np
    import concourse.bacc as _bacc
    from concourse import mybir as _mybir
    from concourse.bass_utils import run_bass_kernel_spmd as _run

    nc = _bacc.Bacc("TRN2", target_bir_lowering=False, num_devices=1)
    arrays, args = {}, []
    for name in _INS:
        a = _np.ascontiguousarray(inputs[name])
        arrays[f"in_{name}"] = a
        args.append(nc.dram_tensor(f"in_{name}", a.shape, _mybir.dt.from_np(a.dtype), kind="ExternalInput").ap())
    table = constants()[0]
    arrays["in_constants"] = table
    args.append(nc.dram_tensor("in_constants", table.shape, _mybir.dt.float32, kind="ExternalInput").ap())
    args.append(nc.dram_tensor("out", (B, S, D), _mybir.dt.float32, kind="ExternalOutput").ap())
    build(nc, *args)
    r = _run(nc, [arrays], core_ids=[0])
    return r.results[0]["out"]
```
